# Optimizing a Trainium2 kernel written in Bass

```python
import numpy as np
import jax
import jax.numpy as jnp

def _softmax(x, axis=-1):
    return jax.nn.softmax(x, axis=axis)

def _gelu(x):
    return jax.nn.gelu(x, approximate=True)

def _silu(x):
    return jax.nn.silu(x)

def _sigmoid(x):
    return jax.nn.sigmoid(x)

def _layernorm(x, axis=-1, eps=1e-05):
    m = jnp.mean(x, axis=axis, keepdims=True)
    v = jnp.var(x, axis=axis, keepdims=True)
    return (x - m) / jnp.sqrt(v + eps)

def _scatter_add(tgt, idx, src, axis=0):
    return tgt.at[idx].add(src)

def _segment_sum(src, seg, n):
    return jax.ops.segment_sum(src, seg, n)
kernel_name = 'mk_adaln_ffn_d1_seqx_r4_25146e'

def setup_inputs(seed: int=0):
    np.random.seed(seed)
    _w = jnp.asarray

    def _rec_inputs():
        import jax
        import jax.numpy as jnp
        _rk = jax.random.key(seed)
        x = -0.0003929 + 0.9999 * jax.random.normal(jax.random.fold_in(_rk, 1), (2, 1024, 256), jnp.float32)
        _lenS = 1024 - jax.random.randint(jax.random.fold_in(_rk, 7), (2,), 0, max(1, 1024 // 4) + 1, jnp.int32)
        _lenS2 = 1024 - jax.random.randint(jax.random.fold_in(_rk, 8), (2,), 0, max(1, 1024 // 4) + 1, jnp.int32)
        fside_Bx1x1024x16_0 = 0.00222621 + 0.99962 * jax.random.normal(jax.random.fold_in(_rk, 11), (2, 1, 256, 16), jnp.float32)
        cond_1024 = -0.00745576 + 0.997402 * jax.random.normal(jax.random.fold_in(_rk, 12), (2, 256), jnp.float32)
        return (x, fside_Bx1x1024x16_0, cond_1024)
    x, fside_Bx1x1024x16_0, cond_1024 = _rec_inputs()

    def _L0_cond_setup():
        import jax, jax.numpy as jnp
        import numpy as np
        B, F_, IN, OUT, R = (32, 128, 256, 256, 16)
        key = jax.random.key(seed)
        ks = jax.random.split(key, 6)
        x = jax.random.normal(ks[0], (B, F_, IN), dtype=jnp.float32)
        u = jax.random.normal(ks[1], (B, 1, OUT, R), dtype=jnp.float32)
        v = jax.random.normal(ks[2], (B, 1, IN, R), dtype=jnp.float32)
        b = jax.random.normal(ks[3], (B, 1, OUT), dtype=jnp.float32)
        lim = 1.0 / np.sqrt(IN)
        W = jax.random.uniform(ks[4], (OUT, IN), minval=-lim, maxval=lim, dtype=jnp.float32)
        fc_bias = jax.random.uniform(ks[5], (OUT,), minval=-lim, maxval=lim, dtype=jnp.float32)
        return {'x': x, 'u': u, 'v': v, 'b': b, 'W': W, 'fc_bias': fc_bias}
    _L0_cond_all = _L0_cond_setup()
    _L0_cond_in = {k: v for k, v in _L0_cond_all.items() if k in ('W', 'fc_bias')}
    del _L0_cond_all

    def _L0_ffn_setup():
        import jax, jax.numpy as jnp
        import numpy as np
        B, S, H = (4, 512, 256)
        E, K, INTER = (16, 2, 128)
        ALPHA, LIMIT = (1.702, 7.0)
        key = jax.random.key(seed)
        ks = jax.random.split(key, 6)
        return {'hidden_states': jax.random.normal(ks[0], (B, S, H), jnp.float32), 'router_weight': jax.random.normal(ks[1], (H, E), jnp.float32) * 0.02, 'gate_up_proj': jax.random.normal(ks[2], (E, H, 2 * INTER), jnp.float32) * 0.02, 'gate_up_proj_bias': jax.random.normal(ks[3], (E, 2 * INTER), jnp.float32) * 0.02, 'down_proj': jax.random.normal(ks[4], (E, INTER, H), jnp.float32) * 0.02, 'down_proj_bias': jax.random.normal(ks[5], (E, H), jnp.float32) * 0.02}
    _L0_ffn_all = _L0_ffn_setup()
    _L0_ffn_in = {k: v for k, v in _L0_ffn_all.items() if k in ('router_weight', 'gate_up_proj', 'gate_up_proj_bias', 'down_proj', 'down_proj_bias')}
    del _L0_ffn_all
    return {'x': x, 'fside_Bx1x1024x16_0': fside_Bx1x1024x16_0, 'cond_1024': cond_1024, 'L0_cond_W': _L0_cond_in['W'], 'L0_cond_fc_bias': _L0_cond_in['fc_bias'], 'L0_ffn_router_weight': _L0_ffn_in['router_weight'], 'L0_ffn_gate_up_proj': _L0_ffn_in['gate_up_proj'], 'L0_ffn_gate_up_proj_bias': _L0_ffn_in['gate_up_proj_bias'], 'L0_ffn_down_proj': _L0_ffn_in['down_proj'], 'L0_ffn_down_proj_bias': _L0_ffn_in['down_proj_bias']}

def reference(x, fside_Bx1x1024x16_0, cond_1024, L0_cond_W, L0_cond_fc_bias, L0_ffn_router_weight, L0_ffn_gate_up_proj, L0_ffn_gate_up_proj_bias, L0_ffn_down_proj, L0_ffn_down_proj_bias):
    import jax
    import jax.numpy as jnp

    def _L0_cond_ref(x, u, v, b, W, fc_bias):
        import jax, jax.numpy as jnp
        import numpy as np
        B, F_, IN, OUT, R = (32, 128, 256, 256, 16)
        inch = x.shape[-1]
        r = v.shape[-1]
        z1 = jnp.einsum('bfi,bir->bfr', x, v[:, 0]) / inch
        z = jnp.einsum('bfr,bor->bfo', z1, u[:, 0]) / r
        y = jnp.einsum('bfi,oi->bfo', x, W) + fc_bias + z + b
        return jax.nn.gelu(y, approximate=False)

    def _L0_ffn_ref(hidden_states, router_weight, gate_up_proj, gate_up_proj_bias, down_proj, down_proj_bias):
        import jax, jax.numpy as jnp
        import numpy as np
        B, S, H = (4, 512, 256)
        E, K, INTER = (16, 2, 128)
        ALPHA, LIMIT = (1.702, 7.0)
        b, s, h = hidden_states.shape
        x = hidden_states.reshape(-1, h)
        logits = x @ router_weight
        topk_w, topk_i = jax.lax.top_k(logits, K)
        topk_w = jax.nn.softmax(topk_w, axis=-1)
        one_hot = (topk_i[..., None] == jnp.arange(E)[None, None, :]).astype(topk_w.dtype)
        scores = jnp.einsum('tk,tke->te', topk_w, one_hot)
        gu = jnp.einsum('th,ehf->tef', x, gate_up_proj) + gate_up_proj_bias
        gate = gu[..., ::2]
        up = gu[..., 1::2]
        gate = jnp.minimum(gate, LIMIT)
        up = jnp.clip(up, -LIMIT, LIMIT)
        glu = gate * jax.nn.sigmoid(gate * ALPHA)
        act = (up + 1.0) * glu
        out = jnp.einsum('tei,eih,te->th', act, down_proj, scores)
        out = out + jnp.einsum('te,eh->th', scores, down_proj_bias)
        return out.reshape(b, s, h)
    x = x + _L0_ffn_ref(_L0_cond_ref(x, fside_Bx1x1024x16_0, fside_Bx1x1024x16_0, cond_1024[:, None, :], L0_cond_W, L0_cond_fc_bias), L0_ffn_router_weight, L0_ffn_gate_up_proj, L0_ffn_gate_up_proj_bias, L0_ffn_down_proj, L0_ffn_down_proj_bias)
    return x

_drawn_inputs = setup_inputs


def setup_inputs(seed=0):
    import zlib

    import numpy as np

    out = dict(_drawn_inputs(seed))
    spreads = {}
    factors = {'fside_Bx1x1024x16_0': 8.0,
     'L0_cond_W': 2.9,
     'L0_cond_fc_bias': 8.0,
     'L0_ffn_gate_up_proj_bias': 23.601,
     'L0_ffn_down_proj_bias': 4.153}
    for name, (base, spread) in spreads.items():
        noise = np.random.default_rng([zlib.crc32(name.encode()), seed]).standard_normal(out[name].shape)
        drawn = base * np.exp(spread * noise) if base else spread * noise
        out[name] = jnp.asarray(drawn.astype(out[name].dtype))
    for name, factor in factors.items():
        out[name] = (out[name] * factor).astype(out[name].dtype)
    return out
```

```python
import concourse.bass as bass
from concourse import mybir
from contextlib import ExitStack

FP32 = mybir.dt.float32
BF16 = mybir.dt.bfloat16
U32 = mybir.dt.uint32
I32 = mybir.dt.int32
ALU = mybir.AluOpType
ACT = mybir.ActivationFunctionType
AX = mybir.AxisListType

ALPHA, LIMIT = 1.702, 7.0
SIG_MAX = 0.9999933036


def adaln_moe_ffn(nc, x, fside, cond, cond_w, fc_bias, router_w, gate_up, gate_up_bias, down, down_bias, out):
    P = 128
    B, S, H = x.shape
    R = fside.shape[3]
    E, _, F2 = gate_up.shape
    INTER = F2 // 2
    TOPK = 2
    T = B * S
    NT = T // P
    HC = H // P
    GT = 4
    NG = NT // GT
    GPB = NG // B
    MAX_BLOCKS = T * TOPK // P + E - 1
    PAIRS_IN_BODY = 4
    RING = 2 * PAIRS_IN_BODY
    ITERS = -(-MAX_BLOCKS // RING)
    NB = ITERS * RING
    REGION = T + P
    XROWS = E * REGION + P
    RW = H + 1
    SKIP = T * TOPK
    E1 = E + 1

    x_v = x.rearrange("b (t p) h -> p (b t) h", p=P)
    out_v = out.rearrange("b (t p) h -> p (b t) h", p=P)
    xs = nc.dram_tensor("dispatched", (XROWS, RW), FP32, kind="Internal").ap()
    rs = nc.dram_tensor("pair_results", (T * TOPK, H), FP32, kind="Internal").ap()
    rs_v = rs.rearrange("(k t p) h -> p k t h", p=P, k=TOPK)

    ctx = ExitStack()
    with ctx:
        def sb(name, shape, dt=FP32):
            return ctx.enter_context(nc.sbuf_tensor(name, shape, dt))

        def sem(name):
            return ctx.enter_context(nc.semaphore(name))

        x_sb = sb("x_sb", [P, NT, H])
        w_nat = sb("w_nat", [P, HC, H])
        fs_nat = sb("fs_nat", [P, B, HC, R])
        fcb = sb("fcb", [P, HC])
        cnd = sb("cnd", [P, B, HC])
        rw = sb("rw", [P, HC, E])
        wgu = sb("wgu", [P, E * HC * F2])
        wd = sb("wd", [P, E * H])
        bgu = sb("bgu", [1, E * F2])
        bd = sb("bd", [1, E * H])
        ident = sb("ident", [P, P])
        tri = sb("tri", [P, P], BF16)
        trif = sb("trif", [E1, E1])
        ones_b = sb("ones_b", [P, P], BF16)
        ones_f = sb("ones_f", [E1, P])
        iota_e = sb("iota_e", [P, E])
        ebase = sb("ebase", [P, E])
        iota_blk = sb("iota_blk", [E1, NB])
        iota_cnt = sb("iota_cnt", [E1, NT])
        ecol = sb("ecol", [E1, 4])
        pad = sb("pad", [P, RW])
        fsT = sb("fsT", [R, B, H])
        fsTs = sb("fsTs", [R, B, H])
        weff = sb("weff", [P, B, HC, H])
        cbias = sb("cbias", [P, B, HC])
        xT = sb("xT", [P, 2, HC, GT * P])
        yT = sb("yT", [P, 2, HC, GT * P])
        yrow = [sb(f"yrow{k}", [P, NT, RW]) for k in range(TOPK)]
        lg = sb("lg", [P, NT, E])
        top = sb("top", [P, NT, 8])
        topi = sb("topi", [P, NT, 8], U32)
        mask = sb("mask", [P, GT, TOPK, E])
        multi = sb("multi", [P, GT, E1], BF16)
        gsum = sb("gsum", [P, NG, E1], BF16)
        rbase = sb("rbase", [P, GT, E])
        prod = sb("prod", [P, GT, TOPK, E])
        slot = sb("slot", [P, NT, TOPK], U32)
        ldif = sb("ldif", [P, NT])
        score = sb("score", [P, TOPK, NT])
        cnt = sb("cnt", [E1, 1])
        over = sb("over", [E1, NT])
        nblk = sb("nblk", [E1, 1])
        cexc = sb("cexc", [E1, 1])
        cinc = sb("cinc", [E1, 1])
        base = sb("base", [E1, 1])
        started = sb("started", [E1, NB])
        owner = sb("owner", [E1, NB])
        rowat = sb("rowat", [E1, NB])
        rowown = sb("rowown", [E1, NB])
        table = sb("table", [1, 2, NB], I32)
        yg = sb("yg", [P, RING, RW])
        ygT = sb("ygT", [P, 2, 2, HC, P])
        sig = sb("sig", [P, 2, 2, INTER])
        up1 = sb("up1", [P, 2, 2, INTER])
        gup = sb("gup", [P, 2, 2, INTER])
        act = sb("act", [P, 2, 2, INTER])
        actT = sb("actT", [P, 2, 2, P])
        res = sb("res", [P, RING, H])
        rin = yrow[0][:, :, :].rearrange("p t h -> p (t h)")[:, 0:NT * H].rearrange(
            "p (b k t h) -> p b k t h", b=2, k=TOPK, t=GT)
        part = sb("part", [P, 2, H])
        osb = yrow[1][:, :, :].rearrange("p t h -> p (t h)")[:, 0:NT * H].rearrange("p (t h) -> p t h", t=NT)

        bank = [ctx.enter_context(nc.psum_tensor(f"bank{i}", [P, 512], FP32)) for i in range(8)]

        s_const = sem("s_const")
        s_dest = sem("s_dest")
        s_in = sem("s_in")
        s_bias_in = sem("s_bias_in")
        s_router_in = sem("s_router_in")
        s_x = [sem(f"s_x{g}") for g in range(NG)]
        s_wgu = sem("s_wgu")
        s_eb = sem("s_eb")
        s_prefill = sem("s_prefill")
        s_fsT_ps = sem("s_fsT_ps")
        s_fsT = sem("s_fsT")
        s_weff_ps = sem("s_weff_ps")
        s_weff = sem("s_weff")
        s_cbias = sem("s_cbias")
        s_xT_ps = sem("s_xT_ps")
        s_xT = sem("s_xT")
        s_cond = sem("s_cond")
        s_yT = sem("s_yT")
        s_lg_ps = sem("s_lg_ps")
        s_lg = sem("s_lg")
        s_yn_ps = sem("s_yn_ps")
        s_yn = sem("s_yn")
        s_yn2 = sem("s_yn2")
        s_gsum = sem("s_gsum")
        s_rank = sem("s_rank")
        s_slot = sem("s_slot")
        s_v = sem("s_v")
        s_scattered = sem("s_scattered")
        s_cnt = sem("s_cnt")
        s_nblk = sem("s_nblk")
        s_pre = sem("s_pre")
        s_own = sem("s_own")
        s_tab_ps = sem("s_tab_ps")
        s_table = sem("s_table")
        s_biasrow = sem("s_biasrow")
        s_yg = [sem(f"s_yg{s}") for s in range(RING)]
        s_ygT_ps = sem("s_ygT_ps")
        s_ygT = sem("s_ygT")
        s_gu = sem("s_gu")
        s_sig = sem("s_sig")
        s_act = sem("s_act")
        s_actT_ps = sem("s_actT_ps")
        s_actT = sem("s_actT")
        s_dn = sem("s_dn")
        s_res = sem("s_res")
        s_stored = [sem(f"s_stored{s}") for s in range(RING)]
        s_dv = sem("s_dv")
        s_rin = [sem(f"s_rin{i}") for i in range(2)]
        s_score = sem("s_score")
        s_ldif = sem("s_ldif")
        s_part = sem("s_part")
        s_osb = sem("s_osb")
        s_out = sem("s_out")

        xT_ps = [bank[c] for c in range(HC)]
        cond_ps = [bank[2 + c] for c in range(HC)]
        lg_ps = bank[4][:, 0:GT * E].rearrange("p (t e) -> p t e", t=GT)
        rank_ps = bank[5][:, 0:GT * E].rearrange("p (t e) -> p t e", t=GT)
        yn_ps = [bank[6 + i][:, :].rearrange("p (t h) -> p t h", t=2) for i in range(2)]
        ygT_ps = [bank[i][:, :].rearrange("p (j c s) -> p j c s", j=2, c=HC) for i in range(2)]
        gu_ps = [bank[2 + i][:, :].rearrange("p (j f) -> p j f", j=2) for i in range(2)]
        actT_ps = [bank[4 + i][:, 0:2 * P].rearrange("p (j s) -> p j s", j=2) for i in range(2)]
        dn_ps = [bank[6 + i][:, :].rearrange("p (j h) -> p j h", j=2) for i in range(2)]

        block = ctx.enter_context(nc.Block())

        def need(eng, semaphore, value):
            if not isinstance(value, int) or value > 0:
                eng.wait_ge(semaphore, value)

        @block.sync
        def _(sp):
            sp.dma_start(fs_nat[:, :, :, :], fside.rearrange("b a (c p) r -> p (b a) c r", p=P)).then_inc(s_in, 16)
            sp.dma_start(w_nat[:, :, :], cond_w.rearrange("(c p) i -> p c i", p=P)).then_inc(s_in, 16)
            for g in range(NG):
                sp.dma_start(x_sb[:, g * GT:(g + 1) * GT, :], x_v[:, g * GT:(g + 1) * GT, :]).then_inc(s_x[g], 16)
            sp.dma_start(wgu[:, :].rearrange("p (e c f) -> p e c f", e=E, c=HC),
                         gate_up.rearrange("e (c p) f -> p e c f", p=P)).then_inc(s_wgu, 16)
            sp.dma_start(wd[:, :].rearrange("p (e h) -> p e h", e=E),
                         down.rearrange("e p h -> p e h")).then_inc(s_wgu, 16)

            sp.wait_ge(s_scattered, 16 * NT * TOPK)
            sp.wait_ge(s_prefill, 16 * E1)
            sp.wait_ge(s_table, 1)

            def load_blocks(i):
                for s in range(RING):
                    row = sp.value_load(table[0:1, 0, bass.ds(i * RING + s, 1)], min_val=0, max_val=XROWS - P)
                    need(sp, s_stored[s], i * 16)
                    sp.dma_start(yg[:, s, :], xs[bass.ds(row, P), :]).then_inc(s_yg[s], 16)

            load_blocks(0)
            with sp.Fori(1, ITERS) as i:
                load_blocks(i)

            for s in range(RING):
                sp.wait_ge(s_stored[s], 16 * ITERS)
            for g in range(NG):
                if g >= 2:
                    sp.wait_ge(s_osb, (g - 1) * GT)
                for k in range(TOPK):
                    sp.dma_start(rin[:, g % 2, k], rs_v[:, k, g * GT:(g + 1) * GT, :]).then_inc(s_rin[g % 2], 16)

        @block.gpsimd
        def _(pool):
            nc.gpsimd.memset(ident[:, :], 0.0).then_inc(s_const, 1)
            nc.gpsimd.memset(tri[:, :], 1.0).then_inc(s_const, 1)
            nc.gpsimd.memset(trif[:, :], 1.0).then_inc(s_const, 1)
            nc.gpsimd.memset(ones_b[:, :], 1.0).then_inc(s_const, 1)
            nc.gpsimd.memset(ones_f[:, :], 1.0).then_inc(s_const, 1)
            nc.gpsimd.memset(ecol[:, :], 0.0).then_inc(s_const, 1)
            nc.gpsimd.memset(pad[:, 0:H], 0.0).then_inc(s_const, 1)
            nc.gpsimd.iota(pad[:, H:RW].bitcast(I32), pattern=[[0, 1]], base=SKIP, channel_multiplier=0).then_inc(s_const, 1)
            nc.gpsimd.iota(iota_e[:, :], pattern=[[1, E]], base=0, channel_multiplier=0,
                           allow_small_or_imprecise_dtypes=True).then_inc(s_const, 1)
            nc.gpsimd.iota(ebase[:, :], pattern=[[REGION, E]], base=P, channel_multiplier=0,
                           allow_small_or_imprecise_dtypes=True).then_inc(s_const, 1)
            nc.gpsimd.iota(iota_blk[:, :], pattern=[[1, NB]], base=0, channel_multiplier=0,
                           allow_small_or_imprecise_dtypes=True).then_inc(s_const, 1)
            nc.gpsimd.iota(iota_cnt[:, :], pattern=[[P, NT]], base=0, channel_multiplier=0,
                           allow_small_or_imprecise_dtypes=True).then_inc(s_const, 1)
            pool.wait_ge(s_const, 12)
            nc.gpsimd.affine_select(out=ident[:, :], in_=ident[:, :], compare_op=ALU.not_equal, fill=1.0,
                                    base=0, pattern=[[-1, P]], channel_multiplier=1).then_inc(s_const, 1)
            nc.gpsimd.affine_select(out=tri[:, :], in_=tri[:, :], compare_op=ALU.is_gt, fill=0.0,
                                    base=0, pattern=[[1, P]], channel_multiplier=-1).then_inc(s_const, 1)
            nc.gpsimd.affine_select(out=trif[:, :], in_=trif[:, :], compare_op=ALU.is_gt, fill=0.0,
                                    base=0, pattern=[[1, E1]], channel_multiplier=-1).then_inc(s_const, 1)
            nc.gpsimd.iota(ecol[:, 0:1], pattern=[[0, 1]], base=0, channel_multiplier=REGION,
                           allow_small_or_imprecise_dtypes=True).then_inc(s_const, 1)
            nc.gpsimd.affine_select(out=ecol[:, 1:2], in_=ecol[:, 1:2], compare_op=ALU.is_ge, fill=float(P),
                                    base=-E, pattern=[[0, 1]], channel_multiplier=1).then_inc(s_const, 1)
            nc.gpsimd.iota(ecol[:, 2:3], pattern=[[0, 1]], base=0, channel_multiplier=1,
                           allow_small_or_imprecise_dtypes=True).then_inc(s_const, 1)
            nc.gpsimd.affine_select(out=ecol[:, 3:4], in_=ecol[:, 3:4], compare_op=ALU.is_gt, fill=float(NB),
                                    base=E, pattern=[[0, 1]], channel_multiplier=-1).then_inc(s_const, 1)
            pool.wait_ge(s_const, 19)
            nc.gpsimd.affine_select(out=ecol[:, 2:3], in_=ecol[:, 2:3], compare_op=ALU.is_gt, fill=0.0,
                                    base=E, pattern=[[0, 1]], channel_multiplier=-1).then_inc(s_const, 1)
            for k in range(TOPK):
                nc.gpsimd.iota(yrow[k][:, :, H].bitcast(I32), pattern=[[P, NT]], base=k * T,
                               channel_multiplier=1).then_inc(s_dest, 1)
            pool.wait_ge(s_dest, TOPK)

            for g in range(NG):
                pool.wait_ge(s_slot, g + 1)
                pool.wait_ge(s_yn, 2 * (g + 1))
                pool.wait_ge(s_yn2, g + 1)
                for t in range(g * GT, (g + 1) * GT):
                    for k in range(TOPK):
                        nc.gpsimd.indirect_dma_start(
                            out=xs, out_offset=bass.IndirectOffsetOnAxis(ap=slot[:, t, k:k + 1], axis=0),
                            in_=yrow[k][:, t, :], in_offset=None).then_inc(s_scattered, 16)

            last_row = pool.to_reg(T * TOPK - 1)
            pairs_wanted = pool.alloc_register("pairs_wanted")
            pool.reg_mov(pairs_wanted, 0)

            def store_blocks():
                for s in range(RING):
                    if s % 2 == 0:
                        pool.reg_add(pairs_wanted, pairs_wanted, 1)
                    pool.wait_ge(s_dest, TOPK)
                    pool.wait_ge(s_res, pairs_wanted)
                    nc.gpsimd.indirect_dma_start(
                        out=rs, out_offset=bass.IndirectOffsetOnAxis(ap=yg[:, s, H:RW].bitcast(U32), axis=0),
                        in_=res[:, s, :], in_offset=None,
                        bounds_check=last_row, oob_is_err=False).then_inc(s_stored[s], 16)

            with pool.Fori(0, ITERS):
                store_blocks()

        @block.scalar
        def _(act_e):
            act_e.dma_start(fcb[:, :], fc_bias.rearrange("(c p) -> p c", p=P),
                            allow_slow_non_contiguous=True).then_inc(s_bias_in, 16)
            for b in range(B):
                act_e.dma_start(cnd[:, b, :], cond[b, :].rearrange("(c p) -> p c", p=P),
                                allow_slow_non_contiguous=True).then_inc(s_bias_in, 16)
            act_e.dma_start(rw[:, :, :], router_w.rearrange("(c p) e -> p c e", p=P)).then_inc(s_router_in, 16)
            act_e.dma_start(bgu[:, :], gate_up_bias.rearrange("(a e) f -> a (e f)", a=1)).then_inc(s_eb, 16)
            act_e.dma_start(bd[:, :], down_bias.rearrange("(a e) f -> a (e f)", a=1)).then_inc(s_eb, 16)
            act_e.wait_ge(s_const, 12)
            for e in range(E1):
                act_e.dma_start(xs[e * REGION:e * REGION + P, :], pad[:, :]).then_inc(s_prefill, 16)

            act_e.wait_ge(s_cbias, 1)
            for g in range(NG):
                for oc in range(HC):
                    act_e.wait_ge(s_cond, g * HC + oc + 1)
                    if g >= 2 and oc == 0:
                        act_e.wait_ge(s_yn_ps, 2 * (g - 1))
                    nc.scalar.activation(yT[:, g % 2, oc, :], cond_ps[oc][:, :], ACT.Gelu,
                                         bias=cbias[:, g // GPB, oc:oc + 1]).then_inc(s_yT, 1)
                for h in range(2):
                    act_e.wait_ge(s_yn_ps, 2 * g + h + 1)
                    t = g * GT + 2 * h
                    nc.scalar.activation(yrow[0][:, t:t + 2, 0:H], yn_ps[h], ACT.Copy).then_inc(s_yn, 1)
            act_e.wait_ge(s_ldif, 1)
            nc.scalar.activation(score[:, 0, :], ldif[:, :], ACT.Sigmoid).then_inc(s_score, 1)
            nc.scalar.activation(score[:, 1, :], ldif[:, :], ACT.Sigmoid, scale=-1.0).then_inc(s_score, 1)

            def copy_ygT(p, u):
                act_e.wait_ge(s_ygT_ps, p + 1)
                need(act_e, s_gu, p - 1)
                nc.scalar.activation(ygT[:, u % 2], ygT_ps[u % 2], ACT.Copy).then_inc(s_ygT, 1)

            def sigmoid(p, u):
                act_e.wait_ge(s_gu, p + 1)
                need(act_e, s_act, p - 1)
                nc.scalar.activation(sig[:, u % 2], gu_ps[u % 2][:, :, 0:F2:2], ACT.Sigmoid,
                                     scale=ALPHA).then_inc(s_sig, 1)

            def copy_res(p, u, stored, so_far):
                act_e.wait_ge(s_dn, p + 1)
                for s in (2 * u, 2 * u + 1):
                    need(act_e, s_stored[s], so_far)
                nc.scalar.activation(res[:, 2 * u:2 * u + 2, :], dn_ps[u % 2], ACT.Copy).then_inc(s_res, 1)

            def experts(i):
                for u in range(PAIRS_IN_BODY):
                    p = i * PAIRS_IN_BODY + u
                    copy_ygT(p, u)
                    sigmoid(p, u)
                    if u >= 1:
                        copy_res(p - 1, u - 1, s_stored, 16 * i)
                    elif not isinstance(i, int) or i >= 1:
                        copy_res(p - 1, PAIRS_IN_BODY - 1, s_stored, 16 * i - 16)

            experts(0)
            experts(1)
            with act_e.Fori(2, ITERS) as i:
                experts(i)
            copy_res(ITERS * PAIRS_IN_BODY - 1, PAIRS_IN_BODY - 1, s_stored, 16 * (ITERS - 1))

            for t in range(NT):
                act_e.wait_ge(s_osb, t + 1)
                act_e.dma_start(out_v[:, t, :], osb[:, t, :]).then_inc(s_out, 16)
            act_e.wait_ge(s_out, 16 * NT)

        @block.tensor
        def _(pe):
            pe.wait_ge(s_const, 20)
            pe.wait_ge(s_in, 32)
            for b in range(B):
                for c in range(HC):
                    last = nc.tensor.matmul(bank[4][0:R, (b * HC + c) * P:(b * HC + c + 1) * P],
                                            fs_nat[:, b, c, :], ident[:, :], start=True, stop=True)
            last.then_inc(s_fsT_ps, 1)
            pe.wait_ge(s_fsT, 2)
            for b in range(B):
                for ic in range(HC):
                    for oc in range(HC):
                        o = cond_ps[b][:, ic * H + oc * P:ic * H + (oc + 1) * P]
                        nc.tensor.matmul(o, w_nat[:, oc, ic * P:(ic + 1) * P], ident[:, :], start=True, stop=False)
                        last = nc.tensor.matmul(o, fsTs[:, b, ic * P:(ic + 1) * P], fsT[:, b, oc * P:(oc + 1) * P],
                                                start=False, stop=True)
                last.then_inc(s_weff_ps, 1)

            def transpose_x(g):
                pe.wait_ge(s_x[g], 16)
                for c in range(HC):
                    if g >= 1:
                        pe.wait_ge(s_xT, (g - 1) * HC + c + 1)
                    for q in range(GT):
                        last = nc.tensor.transpose(xT_ps[c][:, q * P:(q + 1) * P],
                                                   x_sb[:, g * GT + q, c * P:(c + 1) * P], ident[:, :])
                    last.then_inc(s_xT_ps, 1)

            def cond_product(g):
                pe.wait_ge(s_xT, (g + 1) * HC)
                for oc in range(HC):
                    if g >= 1:
                        pe.wait_ge(s_yT, (g - 1) * HC + oc + 1)
                    for ic in range(HC):
                        last = nc.tensor.matmul(cond_ps[oc][:, :], weff[:, g // GPB, ic, oc * P:(oc + 1) * P],
                                                xT[:, g % 2, ic, :], start=(ic == 0), stop=(ic == HC - 1))
                    last.then_inc(s_cond, 1)

            def logits(g):
                pe.wait_ge(s_yT, (g + 1) * HC)
                if g >= 1:
                    pe.wait_ge(s_lg, g)
                for q in range(GT):
                    for c in range(HC):
                        last = nc.tensor.matmul(lg_ps[:, q, :], yT[:, g % 2, c, q * P:(q + 1) * P], rw[:, c, :],
                                                start=(c == 0), stop=(c == HC - 1))
                last.then_inc(s_lg_ps, 1)

            def y_by_token(g):
                for h in range(2):
                    if g >= 1:
                        pe.wait_ge(s_yn, 2 * (g - 1) + h + 1)
                    for j in range(2):
                        q = 2 * h + j
                        for c in range(HC):
                            last = nc.tensor.transpose(yn_ps[h][:, j, c * P:(c + 1) * P],
                                                       yT[:, g % 2, c, q * P:(q + 1) * P], ident[:, :])
                    last.then_inc(s_yn_ps, 1)

            def ranks(g):
                pe.wait_ge(s_gsum, g + 1)
                if g >= 1:
                    pe.wait_ge(s_slot, g)
                nc.tensor.matmul(rank_ps, tri[:, :], multi[:, :, 0:E], start=True, stop=False)
                for q in range(GT - 1):
                    n = GT - 1 - q
                    last = nc.tensor.matmul(rank_ps[:, q + 1:GT, :], ones_b[:, :],
                                            multi[:, q:q + 1, 0:E].broadcast_to([P, n, E]),
                                            start=False, stop=(g == 0 and q == GT - 2))
                for j in range(g):
                    last = nc.tensor.matmul(rank_ps, ones_b[:, :], gsum[:, j:j + 1, 0:E].broadcast_to([P, GT, E]),
                                            start=False, stop=(j == g - 1))
                last.then_inc(s_rank, 1)

            transpose_x(0)
            pe.wait_ge(s_weff, B)
            pe.wait_ge(s_router_in, 16)
            for g in range(NG):
                cond_product(g)
                if g + 1 < NG:
                    transpose_x(g + 1)
                if g >= 1:
                    ranks(g - 1)
                logits(g)
                y_by_token(g)
            ranks(NG - 1)

            pe.wait_ge(s_slot, NG)
            for g in range(NG):
                last = nc.tensor.matmul(bank[5][0:E1, 128:129], gsum[:, g, :], ones_b[:, 0:1],
                                        start=(g == 0), stop=(g == NG - 1))
            last.then_inc(s_cnt, 1)
            pe.wait_ge(s_nblk, 1)
            nc.tensor.matmul(bank[5][0:E1, 136:137], trif[:, :], nblk[:, :], start=True, stop=True).then_inc(s_pre, 1)
            pe.wait_ge(s_own, 1)
            nc.tensor.matmul(bank[5][0:1, 144:144 + NB], ones_f[:, 0:1], rowown[:, :], start=True, stop=True)
            nc.tensor.matmul(bank[5][0:1, 208:208 + NB], ecol[:, 2:3], owner[:, :],
                             start=True, stop=True).then_inc(s_tab_ps, 1)

            pe.wait_ge(s_table, 1)
            pe.wait_ge(s_wgu, 32)
            pe.wait_ge(s_biasrow, 1)
            pe.wait_ge(s_yn, 2 * NG)

            def transpose_y(p, u, so_far):
                need(pe, s_ygT, p - 1)
                for j in range(2):
                    s = 2 * u + j
                    pe.wait_ge(s_yg[s], so_far)
                    for c in range(HC):
                        last = nc.tensor.transpose(ygT_ps[u % 2][:, j, c, :], yg[:, s, c * P:(c + 1) * P],
                                                   ident[:, :])
                last.then_inc(s_ygT_ps, 1)

            def expert_of(i, s):
                return pe.value_load(table[0:1, 1, bass.ds(i * RING + s, 1)], min_val=0, max_val=E - 1)

            def gate_up_product(p, u, experts):
                pe.wait_ge(s_ygT, p + 1)
                need(pe, s_act, p - 1)
                for j in range(2):
                    e = experts[j]
                    o = gu_ps[u % 2][:, j, :]
                    nc.tensor.matmul(o, ones_f[0:1, :], bgu[0:1, bass.ds(e * F2, F2)], start=True, stop=False)
                    for c in range(HC):
                        last = nc.tensor.matmul(o, ygT[:, u % 2, j, c, :],
                                                wgu[:, bass.ds(e * (HC * F2) + c * F2, F2)],
                                                start=False, stop=(c == HC - 1))
                last.then_inc(s_gu, 1)

            def transpose_act(p, u):
                pe.wait_ge(s_act, p + 1)
                need(pe, s_actT, p - 1)
                for j in range(2):
                    last = nc.tensor.transpose(actT_ps[u % 2][:, j, :], act[:, u % 2, j, :], ident[:, :])
                last.then_inc(s_actT_ps, 1)

            def down_product(p, u, experts):
                pe.wait_ge(s_actT, p + 1)
                need(pe, s_res, p - 1)
                for j in range(2):
                    e = experts[j]
                    o = dn_ps[u % 2][:, j, :]
                    nc.tensor.matmul(o, ones_f[0:1, :], bd[0:1, bass.ds(e * H, H)], start=True, stop=False)
                    last = nc.tensor.matmul(o, actT[:, u % 2, j, :], wd[:, bass.ds(e * H, H)], start=False, stop=True)
                last.then_inc(s_dn, 1)

            def experts(i, first=False):
                for u in range(PAIRS_IN_BODY):
                    p = i * PAIRS_IN_BODY + u
                    transpose_y(p, u, 16 * i + 16)
                    ex = [expert_of(i, 2 * u + j) for j in range(2)]
                    gate_up_product(p, u, ex)
                    if not (first and u == 0):
                        v = (u - 1) % PAIRS_IN_BODY
                        before = [expert_of(i if u else i - 1, 2 * v + j) for j in range(2)]
                        transpose_act(p - 1, v)
                        down_product(p - 1, v, before)

            experts(0, first=True)
            with pe.Fori(1, ITERS) as i:
                experts(i)
            v = PAIRS_IN_BODY - 1
            before = [expert_of(ITERS - 1, 2 * v + j) for j in range(2)]
            transpose_act(ITERS * PAIRS_IN_BODY - 1, v)
            down_product(ITERS * PAIRS_IN_BODY - 1, v, before)

        @block.vector
        def _(dve):
            own_steps = [0]

            def after(ins):
                own_steps[0] += 1
                ins.then_inc(s_v, 1)
                dve.wait_ge(s_v, own_steps[0])

            dve.wait_ge(s_fsT_ps, 1)
            nc.vector.tensor_copy(fsT[:, :, :], bank[4][0:R, :].rearrange("r (b h) -> r b h", b=B)).then_inc(s_fsT, 1)
            nc.vector.tensor_scalar(fsTs[:, :, :], bank[4][0:R, :].rearrange("r (b h) -> r b h", b=B),
                                    1.0 / (H * R), None, ALU.mult).then_inc(s_fsT, 1)
            dve.wait_ge(s_bias_in, 16 * (1 + B))
            for b in range(B):
                last = nc.vector.tensor_tensor(cbias[:, b, :], cnd[:, b, :], fcb[:, :], ALU.add)
            last.then_inc(s_cbias, 1)
            for b in range(B):
                dve.wait_ge(s_weff_ps, b + 1)
                nc.vector.tensor_copy(weff[:, b, :, :], cond_ps[b][:, :].rearrange("p (c h) -> p c h", c=HC)).then_inc(s_weff, 1)
            dve.wait_ge(s_eb, 32)
            up_bias = bgu[0:1, 1:E * F2:2]
            nc.vector.tensor_scalar(up_bias, up_bias, 1.0, None, ALU.add).then_inc(s_biasrow, 1)
            nc.vector.memset(multi[:, :, :], 0.0).then_inc(s_dv, 1)
            dve.wait_ge(s_dv, 1)

            def copy_xT(g):
                for c in range(HC):
                    dve.wait_ge(s_xT_ps, g * HC + c + 1)
                    if g >= 2:
                        dve.wait_ge(s_cond, (g - 1) * HC)
                    nc.vector.tensor_copy(xT[:, g % 2, c, :], xT_ps[c][:, :]).then_inc(s_xT, 1)

            def choose(g):
                ts = slice(g * GT, (g + 1) * GT)
                dve.wait_ge(s_lg_ps, g + 1)
                nc.vector.tensor_copy(lg[:, ts, :], lg_ps).then_inc(s_lg, 1)
                dve.wait_ge(s_lg, g + 1)
                for t in range(g * GT, (g + 1) * GT):
                    last = nc.vector.max(top[:, t, :], lg[:, t, :])
                after(last)
                for t in range(g * GT, (g + 1) * GT):
                    last = nc.vector.max_index(topi[:, t, :], top[:, t, :], lg[:, t, :])
                after(last)
                if g >= 1:
                    dve.wait_ge(s_rank, g)
                after(nc.vector.tensor_tensor(
                    mask[:, :, :, :], topi[:, ts, 0:TOPK].unsqueeze(3).broadcast_to([P, GT, TOPK, E]),
                    iota_e[:, :].unsqueeze(1).unsqueeze(1).broadcast_to([P, GT, TOPK, E]), ALU.is_equal))
                after(nc.vector.tensor_tensor(multi[:, :, 0:E], mask[:, :, 0, :], mask[:, :, 1, :], ALU.add))
                with nc.allow_low_precision("counts up to 8 are exact"):
                    nc.vector.tensor_reduce(gsum[:, g, :], multi[:, :, :].rearrange("p t e -> p e t"),
                                            axis=AX.X, op=ALU.add).then_inc(s_gsum, 1)

            def place(g):
                ts = slice(g * GT, (g + 1) * GT)
                dve.wait_ge(s_rank, g + 1)
                after(nc.vector.tensor_tensor(rbase[:, :, :], rank_ps,
                                              ebase[:, :].unsqueeze(1).broadcast_to([P, GT, E]), ALU.add))
                after(nc.vector.tensor_tensor(prod[:, :, :, :], mask[:, :, :, :],
                                              rbase[:, :, :].unsqueeze(2).broadcast_to([P, GT, TOPK, E]), ALU.mult))
                with nc.allow_low_precision("row numbers are integers below 2^24"):
                    nc.vector.tensor_reduce(slot[:, ts, :], prod[:, :, :, :], axis=AX.X, op=ALU.add).then_inc(s_slot, 1)

            copy_xT(0)
            dve.wait_ge(s_dest, TOPK)
            for g in range(NG):
                if g + 1 < NG:
                    copy_xT(g + 1)
                choose(g)
                place(g)
                dve.wait_ge(s_yn, 2 * (g + 1))
                ts = slice(g * GT, (g + 1) * GT)
                nc.vector.tensor_copy(yrow[1][:, ts, 0:H], yrow[0][:, ts, 0:H]).then_inc(s_yn2, 1)
            nc.vector.tensor_tensor(ldif[:, :], top[:, :, 0], top[:, :, 1], ALU.subtract).then_inc(s_ldif, 1)

            dve.wait_ge(s_cnt, 1)
            after(nc.vector.tensor_copy(cnt[:, :], bank[5][0:E1, 128:129]))
            after(nc.vector.tensor_scalar(over[:, :], iota_cnt[:, :], cnt[:, 0:1], None, ALU.is_lt))
            after(nc.vector.tensor_reduce(nblk[:, :], over[:, :], axis=AX.X, op=ALU.add))
            nc.vector.tensor_tensor(nblk[:, :], nblk[:, :], ecol[:, 3:4], ALU.add).then_inc(s_nblk, 1)
            dve.wait_ge(s_pre, 1)
            after(nc.vector.tensor_copy(cexc[:, :], bank[5][0:E1, 136:137]))
            after(nc.vector.tensor_tensor(cinc[:, :], cexc[:, :], nblk[:, :], ALU.add))
            after(nc.vector.tensor_tensor(base[:, :], cexc[:, :], ecol[:, 1:2], ALU.mult))
            after(nc.vector.tensor_tensor(base[:, :], base[:, :], cnt[:, :], ALU.add))
            after(nc.vector.tensor_tensor(base[:, :], base[:, :], ecol[:, 0:1], ALU.add))
            after(nc.vector.tensor_scalar(started[:, :], iota_blk[:, :], cexc[:, 0:1], None, ALU.is_ge))
            after(nc.vector.scalar_tensor_tensor(owner[:, :], iota_blk[:, :], cinc[:, 0:1], started[:, :],
                                                 ALU.is_lt, ALU.mult))
            after(nc.vector.tensor_scalar(rowat[:, :], iota_blk[:, :], ecol[:, 1:2], base[:, 0:1],
                                          ALU.mult, ALU.subtract))
            nc.vector.scalar_tensor_tensor(rowown[:, :], rowat[:, :], -1.0, owner[:, :],
                                           ALU.mult, ALU.mult).then_inc(s_own, 1)
            dve.wait_ge(s_tab_ps, 1)
            after(nc.vector.tensor_copy(table[0:1, 0, :], bank[5][0:1, 144:144 + NB]))
            nc.vector.tensor_copy(table[0:1, 1, :], bank[5][0:1, 208:208 + NB]).then_inc(s_table, 1)

            def activate(p, u):
                b = u % 2
                dve.wait_ge(s_sig, p + 1)
                nc.vector.tensor_scalar(up1[:, b], gu_ps[b][:, :, 1:F2:2], 1.0 - LIMIT, 1.0 + LIMIT,
                                        ALU.max, ALU.min).then_inc(s_dv, 1)
                dve.wait_ge(s_dv, 2 * p + 2)
                need(dve, s_actT_ps, p - 1)
                nc.vector.scalar_tensor_tensor(gup[:, b], gu_ps[b][:, :, 0:F2:2], LIMIT, up1[:, b],
                                               ALU.min, ALU.mult).then_inc(s_dv, 1)
                dve.wait_ge(s_dv, 2 * p + 3)
                nc.vector.scalar_tensor_tensor(act[:, b], sig[:, b], SIG_MAX, gup[:, b],
                                               ALU.min, ALU.mult).then_inc(s_act, 1)

            def copy_actT(p, u):
                dve.wait_ge(s_actT_ps, p + 1)
                need(dve, s_dn, p - 1)
                nc.vector.tensor_copy(actT[:, u % 2], actT_ps[u % 2]).then_inc(s_actT, 1)

            def experts(i):
                for u in range(PAIRS_IN_BODY):
                    p = i * PAIRS_IN_BODY + u
                    activate(p, u)
                    copy_actT(p, u)

            experts(0)
            with dve.Fori(1, ITERS) as i:
                experts(i)

            dve.wait_ge(s_score, 2)
            for g in range(NG):
                dve.wait_ge(s_rin[g % 2], 16 * TOPK * (g // 2 + 1))
                for q in range(GT):
                    t = g * GT + q
                    nc.vector.scalar_tensor_tensor(part[:, t % 2, :], rin[:, g % 2, 0, q, :], score[:, 0, t:t + 1],
                                                   x_sb[:, t, :], ALU.mult, ALU.add).then_inc(s_part, 1)
                    dve.wait_ge(s_part, t + 1)
                    nc.vector.scalar_tensor_tensor(osb[:, t, :], rin[:, g % 2, 1, q, :], score[:, 1, t:t + 1],
                                                   part[:, t % 2, :], ALU.mult, ALU.add).then_inc(s_osb, 1)


_INS = ["x", "fside_Bx1x1024x16_0", "cond_1024", "L0_cond_W", "L0_cond_fc_bias", "L0_ffn_router_weight",
        "L0_ffn_gate_up_proj", "L0_ffn_gate_up_proj_bias", "L0_ffn_down_proj", "L0_ffn_down_proj_bias"]


def kernel(**inputs):
    import numpy as np
    import concourse.bacc as bacc
    from concourse.bass_utils import run_bass_kernel_spmd

    nc = bacc.Bacc("TRN2", target_bir_lowering=False, num_devices=1)
    arrays, args = {}, []
    for name in _INS:
        a = np.ascontiguousarray(inputs[name])
        arrays[f"in_{name}"] = a
        args.append(nc.dram_tensor(f"in_{name}", a.shape, mybir.dt.from_np(a.dtype), kind="ExternalInput").ap())
    shape = inputs["x"].shape
    out = nc.dram_tensor("out", shape, FP32, kind="ExternalOutput").ap()
    adaln_moe_ffn(nc, *args, out)
    r = run_bass_kernel_spmd(nc, [arrays], core_ids=[0])
    return r.results[0]["out"]
```

```python
import concourse.bass as bass
from concourse import mybir
from contextlib import ExitStack

FP32 = mybir.dt.float32
FP32R = mybir.dt.float32r
BF16 = mybir.dt.bfloat16
U32 = mybir.dt.uint32
I32 = mybir.dt.int32
ALU = mybir.AluOpType
ACT = mybir.ActivationFunctionType
AX = mybir.AxisListType

ALPHA, LIMIT = 1.702, 7.0
SIG_MAX = 0.9999933036


def adaln_moe_ffn(nc, x, fside, cond, cond_w, fc_bias, router_w, gate_up, gate_up_bias, down, down_bias, out):
    P = 128
    B, S, H = x.shape
    R = fside.shape[3]
    E, _, F2 = gate_up.shape
    INTER = F2 // 2
    TOPK = 2
    T = B * S
    NT = T // P
    HC = H // P
    GT = 4
    NG = NT // GT
    GPB = NG // B
    MAX_BLOCKS = T * TOPK // P + E - 1
    PAIRS_IN_BODY = 4
    RING = 2 * PAIRS_IN_BODY
    ITERS = -(-MAX_BLOCKS // RING)
    NB = ITERS * RING
    REGION = T + P
    XROWS = E * REGION + P
    WE = 2
    WARM0, WARM1 = 14, 30
    PARTS = ("hi", "lo")
    SPLIT_AT = (0, 0, WE, 3 * WE, E)
    SPLIT_AFTER = [range(SPLIT_AT[g], SPLIT_AT[g + 1], WE) for g in range(NG)]
    RW = H + 1
    SKIP = T * TOPK
    E1 = E + 1

    x_v = x.rearrange("b (t p) h -> p (b t) h", p=P)
    out_v = out.rearrange("b (t p) h -> p (b t) h", p=P)
    xs = nc.dram_tensor("dispatched", (XROWS, RW), FP32, kind="Internal").ap()
    rs = nc.dram_tensor("pair_results", (T * TOPK, H), FP32, kind="Internal").ap()
    rs_v = rs.rearrange("(k t p) h -> p k t h", p=P, k=TOPK)

    ctx = ExitStack()
    with ctx:
        def sb(name, shape, dt=FP32):
            return ctx.enter_context(nc.sbuf_tensor(name, shape, dt))

        def sem(name):
            return ctx.enter_context(nc.semaphore(name))

        x_sb = sb("x_sb", [P, NT, H])
        fs_nat = sb("fs_nat", [P, B, HC, R])
        fcb = sb("fcb", [P, HC])
        cnd = sb("cnd", [P, B, HC])
        rw = sb("rw", [P, HC, E])
        wgu_raw = sb("wgu_raw", [P, E * HC * F2])
        wd_raw = sb("wd_raw", [P, E * H])
        wgu = {"hi": sb("wgu_hi", [P, E * HC * F2], FP32R), "lo": wgu_raw[:, :].bitcast(FP32R)}
        wd = {"hi": sb("wd_hi", [P, E * H], FP32R), "lo": wd_raw[:, :].bitcast(FP32R)}
        braw = sb("braw", [E, 2, F2])
        bsplit = {part: sb(f"bsplit_{part}", [E, 2, F2], FP32R) for part in PARTS}
        brow = sb("brow", [4, E * F2], FP32R)
        picksf = sb("picksf", [4, 2, P])
        picks = sb("picks", [4, 2, P], FP32R)
        ident = sb("ident", [P, P])
        tri = sb("tri", [P, P], BF16)
        trif = sb("trif", [E1, E1])
        ones_b = sb("ones_b", [P, P], BF16)
        ones_f = sb("ones_f", [E1, P])
        iota_e = sb("iota_e", [P, E])
        ebase = sb("ebase", [P, E])
        iota_blk = sb("iota_blk", [E1, NB])
        iota_cnt = sb("iota_cnt", [E1, NT])
        ecol = sb("ecol", [E1, 4])
        pad = sb("pad", [P, RW])
        room = sb("room", [P, 4, 2 * 2 * INTER])
        w_nat = room[:, 0, :].rearrange("p (c i) -> p c i", c=HC)
        fsT = room[0:R, 1, :].rearrange("r (b h) -> r b h", b=B)
        fsTs = room[0:R, 2, :].rearrange("r (b h) -> r b h", b=B)
        wT = sb("wT", [P, HC, H])
        weff = sb("weff", [P, B, HC, H])
        cbias = sb("cbias", [P, B, HC])
        yrow = sb("yrow", [P, NT, RW])
        lg = sb("lg", [P, NT, E])
        top = sb("top", [P, NT, 8])
        topi = sb("topi", [P, NT, 8], U32)
        mask = sb("mask", [P, GT, TOPK, E])
        multi = sb("multi", [P, GT, E1], BF16)
        gsum = sb("gsum", [P, NG, E1], BF16)
        rbase = sb("rbase", [P, GT, E])
        prod = sb("prod", [P, GT, TOPK, E])
        slot = sb("slot", [P, NT, TOPK], U32)
        ldif = sb("ldif", [P, NT])
        score = sb("score", [P, TOPK, NT])
        cnt = sb("cnt", [E1, 1])
        over = sb("over", [E1, NT])
        nblk = sb("nblk", [E1, 1])
        cexc = sb("cexc", [E1, 1])
        cinc = sb("cinc", [E1, 1])
        base = sb("base", [E1, 1])
        started = sb("started", [E1, NB])
        owner = sb("owner", [E1, NB])
        rowat = sb("rowat", [E1, NB])
        rowown = sb("rowown", [E1, NB])
        table = sb("table", [1, 2, NB], I32)
        yg = sb("yg", [P, RING, RW])
        idx = sb("idx", [P, RING], U32)
        ygT = {part: sb(f"ygT_{part}", [P, 2, 2, HC, P], FP32R) for part in PARTS}
        sig, up1, gup, act = (room[:, n, :].rearrange("p (b j f) -> p b j f", b=2, j=2) for n in range(4))
        actT = {part: sb(f"actT_{part}", [P, 2, 2, P], FP32R) for part in PARTS}
        res = sb("res", [P, RING, H])
        xT = yg[:, :, :].rearrange("p a b -> p (a b)")[:, 0:2 * HC * GT * P].rearrange(
            "p (b c s) -> p b c s", b=2, c=HC)
        yT = res[:, :, :].rearrange("p a b -> p (a b)").rearrange("p (b c s) -> p b c s", b=2, c=HC)
        def second(t):
            return yg[:, t, 0:H] if t < RING else res[:, t - RING, :]

        bank = [ctx.enter_context(nc.psum_tensor(f"bank{i}", [P, 512], FP32)) for i in range(8)]

        s_ident0 = sem("s_ident0")
        s_ident = sem("s_ident")
        s_const = sem("s_const")
        s_pad = sem("s_pad")
        s_dest = sem("s_dest")
        s_in = sem("s_in")
        s_bias_in = sem("s_bias_in")
        s_router_in = sem("s_router_in")
        s_x = [sem(f"s_x{g}") for g in range(NG)]
        s_w = [sem(f"s_w{n}") for n in range(E // WE)]
        s_whi = sem("s_whi")
        s_wlo = sem("s_wlo")
        s_bsplit = sem("s_bsplit")
        s_brow = sem("s_brow")
        s_picks = sem("s_picks")
        s_wT_ps = sem("s_wT_ps")
        s_wT = sem("s_wT")
        s_side_ps = sem("s_side_ps")
        s_eb = sem("s_eb")
        s_prefill = sem("s_prefill")
        s_fsT_ps = sem("s_fsT_ps")
        s_fsT = sem("s_fsT")
        s_weff = sem("s_weff")
        s_cbias = sem("s_cbias")
        s_xT_ps = sem("s_xT_ps")
        s_xT = sem("s_xT")
        s_cond = sem("s_cond")
        s_yT = sem("s_yT")
        s_lg_ps = sem("s_lg_ps")
        s_lg = sem("s_lg")
        s_yn_ps = sem("s_yn_ps")
        s_yn = sem("s_yn")
        s_gsum = sem("s_gsum")
        s_rank = sem("s_rank")
        s_slot = sem("s_slot")
        s_v = sem("s_v")
        s_first = [sem(f"s_first{g}") for g in range(NG)]
        s_second = sem("s_second")
        s_cnt = sem("s_cnt")
        s_nblk = sem("s_nblk")
        s_pre = sem("s_pre")
        s_own = sem("s_own")
        s_tab_ps = sem("s_tab_ps")
        s_table = sem("s_table")
        s_yg = [sem(f"s_yg{u}") for u in range(PAIRS_IN_BODY)]
        s_ygT_ps = sem("s_ygT_ps")
        s_yhi = sem("s_yhi")
        s_ylo = sem("s_ylo")
        s_gu = sem("s_gu")
        s_sig = sem("s_sig")
        s_act = sem("s_act")
        s_actT_ps = sem("s_actT_ps")
        s_ahi = sem("s_ahi")
        s_alo = sem("s_alo")
        s_dn = sem("s_dn")
        s_res = sem("s_res")
        s_stored = [sem(f"s_stored{u}") for u in range(PAIRS_IN_BODY)]
        s_idx = sem("s_idx")
        s_dv = sem("s_dv")
        s_back = [sem(f"s_back{g}") for g in range(NG)]
        s_score = sem("s_score")
        s_ldif = sem("s_ldif")
        s_part = sem("s_part")
        s_sum = sem("s_sum")
        s_out = sem("s_out")

        xT_ps = [bank[c] for c in range(HC)]
        cond_ps = [bank[2 + c] for c in range(HC)]
        lg_ps = bank[4][:, 0:GT * E].rearrange("p (t e) -> p t e", t=GT)
        rank_ps = bank[5][:, 0:GT * E].rearrange("p (t e) -> p t e", t=GT)
        yn_ps = [bank[6 + i][:, :].rearrange("p (t h) -> p t h", t=2) for i in range(2)]
        ygT_ps = [bank[i][:, :].rearrange("p (j c s) -> p j c s", j=2, c=HC) for i in range(2)]
        gu_ps = [bank[2 + i][:, :].rearrange("p (j f) -> p j f", j=2) for i in range(2)]
        actT_ps = [bank[4 + i][:, 0:2 * P].rearrange("p (j s) -> p j s", j=2) for i in range(2)]
        dn_ps = [bank[6 + i][:, :].rearrange("p (j h) -> p j h", j=2) for i in range(2)]

        block = ctx.enter_context(nc.Block())

        def need(eng, semaphore, value):
            if not isinstance(value, int) or value > 0:
                eng.wait_ge(semaphore, value)

        def table_values(engine, row, start, n, top_value):
            return nc.values_load_multi_w_load_instructions(
                table[0:1, row, bass.ds(start, n)], engines=[engine], min_val=0, max_val=top_value,
                skip_runtime_bounds_check_because="the table's rows and experts come from counts that sum to "
                                                  "the number of pairs, whatever the inputs")[1]

        def earlier(i, u, n):
            return (i, u - n) if u >= n else (i - 1, u - n + PAIRS_IN_BODY)

        @block.sync
        def _(sp):
            sp.dma_start(fs_nat[:, :, :, :], fside.rearrange("b a (c p) r -> p (b a) c r", p=P)).then_inc(s_in, 16)
            sp.dma_start(w_nat[:, :, :], cond_w.rearrange("(c p) i -> p c i", p=P)).then_inc(s_in, 16)
            for g in range(NG):
                sp.dma_start(x_sb[:, g * GT:(g + 1) * GT, :], x_v[:, g * GT:(g + 1) * GT, :]).then_inc(s_x[g], 16)
            sp.dma_start(braw[:, 0, :], gate_up_bias).then_inc(s_eb, 16)
            sp.dma_start(braw[:, 1, :], down_bias).then_inc(s_eb, 16)
            def load_weights(e):
                gu, dn = slice(e * HC * F2, (e + WE) * HC * F2), slice(e * H, (e + WE) * H)
                sp.dma_start(wgu_raw[:, gu].rearrange("p (e c f) -> p (e c) f", c=HC, f=F2),
                             gate_up[e:e + WE, :, :].rearrange("e (c p) f -> p (e c) f", p=P)).then_inc(s_w[e // WE], 16)
                sp.dma_start(wd_raw[:, dn].rearrange("p (e h) -> p e h", h=H),
                             down[e:e + WE, :, :].rearrange("e p h -> p e h")).then_inc(s_w[e // WE], 16)

            for e in range(0, 3 * WE, WE):
                load_weights(e)
            sp.wait_ge(s_first[0], 16 * GT)
            for e in range(3 * WE, 5 * WE, WE):
                load_weights(e)
            sp.wait_ge(s_bsplit, 2)
            for row, (part, which) in enumerate((("hi", 0), ("lo", 0), ("hi", 1), ("lo", 1))):
                sp.dma_start(brow[row:row + 1, :].bitcast(FP32).rearrange("a (e f) -> a e f", e=E),
                             bsplit[part][:, which, :].bitcast(FP32)).then_inc(s_brow, 16)
            sp.wait_ge(s_first[1], 16 * GT)
            for e in range(5 * WE, E, WE):
                load_weights(e)
            sp.wait_ge(s_pad, 2)
            sp.wait_ge(s_first[2], 16 * GT)
            sp.dma_start(xs[0:E * REGION, :].rearrange("(e r) c -> r e c", r=REGION)[0:P, :, :],
                         pad[:, :].unsqueeze(1).broadcast_to([P, E, RW])).then_inc(s_prefill, 16)
            sp.dma_start(xs[E * REGION:XROWS, :], pad[:, :]).then_inc(s_prefill, 16)

            for g in range(NG):
                sp.wait_ge(s_first[g], 16 * GT)
            sp.wait_ge(s_second, 16 * NT)
            sp.wait_ge(s_prefill, 32)
            sp.wait_ge(s_table, 1)

            def load_blocks(i):
                rows = table_values(mybir.EngineType.SP, 0, i * RING, RING, XROWS - P)
                for r in range(RING):
                    if r % 2 == 0:
                        need(sp, s_idx, (i - 1) * PAIRS_IN_BODY + r // 2 + 1)
                    sp.dma_start(yg[:, r, :], xs[bass.ds(rows[r], P), :]).then_inc(s_yg[r // 2], 16)

            load_blocks(0)
            with sp.Fori(1, ITERS) as i:
                load_blocks(i)

            for u in range(PAIRS_IN_BODY):
                sp.wait_ge(s_stored[u], 32 * ITERS)
            for g in range(NG):
                ts = slice(g * GT, (g + 1) * GT)
                sp.dma_start(yrow[:, ts, 0:H], rs_v[:, 0, ts, :]).then_inc(s_back[g], 16)
                half, h0 = (yg[:, :, 0:H], g * GT) if g < NG // 2 else (res, g * GT - RING)
                sp.dma_start(half[:, h0:h0 + GT, :], rs_v[:, 1, ts, :]).then_inc(s_back[g], 16)

        @block.gpsimd
        def _(pool):
            nc.gpsimd.memset(ident[:, :], 0.0).then_inc(s_ident0, 1)
            pool.wait_ge(s_ident0, 1)
            nc.gpsimd.affine_select(out=ident[:, :], in_=ident[:, :], compare_op=ALU.not_equal, fill=1.0,
                                    base=0, pattern=[[-1, P]], channel_multiplier=1).then_inc(s_ident, 1)
            nc.gpsimd.memset(pad[:, 0:H], 0.0).then_inc(s_pad, 1)
            nc.gpsimd.iota(pad[:, H:RW].bitcast(I32), pattern=[[0, 1]], base=SKIP, channel_multiplier=0).then_inc(s_pad, 1)
            nc.gpsimd.memset(tri[:, :], 1.0).then_inc(s_const, 1)
            nc.gpsimd.memset(trif[:, :], 1.0).then_inc(s_const, 1)
            nc.gpsimd.memset(ones_b[:, :], 1.0).then_inc(s_const, 1)
            nc.gpsimd.memset(ones_f[:, :], 1.0).then_inc(s_const, 1)
            nc.gpsimd.memset(ecol[:, :], 0.0).then_inc(s_const, 1)
            nc.gpsimd.memset(picksf[:, :, :], 1.0).then_inc(s_const, 1)
            nc.gpsimd.iota(iota_e[:, :], pattern=[[1, E]], base=0, channel_multiplier=0,
                           allow_small_or_imprecise_dtypes=True).then_inc(s_const, 1)
            nc.gpsimd.iota(ebase[:, :], pattern=[[REGION, E]], base=P, channel_multiplier=0,
                           allow_small_or_imprecise_dtypes=True).then_inc(s_const, 1)
            nc.gpsimd.iota(iota_blk[:, :], pattern=[[1, NB]], base=0, channel_multiplier=0,
                           allow_small_or_imprecise_dtypes=True).then_inc(s_const, 1)
            nc.gpsimd.iota(iota_cnt[:, :], pattern=[[P, NT]], base=0, channel_multiplier=0,
                           allow_small_or_imprecise_dtypes=True).then_inc(s_const, 1)
            pool.wait_ge(s_const, 10)
            nc.gpsimd.affine_select(out=tri[:, :], in_=tri[:, :], compare_op=ALU.is_gt, fill=0.0,
                                    base=0, pattern=[[1, P]], channel_multiplier=-1).then_inc(s_const, 1)
            nc.gpsimd.affine_select(out=trif[:, :], in_=trif[:, :], compare_op=ALU.is_gt, fill=0.0,
                                    base=0, pattern=[[1, E1]], channel_multiplier=-1).then_inc(s_const, 1)
            nc.gpsimd.affine_select(out=picksf[:, 0, :], in_=picksf[:, 0, :], compare_op=ALU.is_gt, fill=0.0,
                                    base=2, pattern=[[0, P]], channel_multiplier=-1).then_inc(s_const, 1)
            nc.gpsimd.affine_select(out=picksf[:, 1, :], in_=picksf[:, 1, :], compare_op=ALU.is_ge, fill=0.0,
                                    base=-2, pattern=[[0, P]], channel_multiplier=1).then_inc(s_const, 1)
            nc.gpsimd.iota(ecol[:, 0:1], pattern=[[0, 1]], base=0, channel_multiplier=REGION,
                           allow_small_or_imprecise_dtypes=True).then_inc(s_const, 1)
            nc.gpsimd.affine_select(out=ecol[:, 1:2], in_=ecol[:, 1:2], compare_op=ALU.is_ge, fill=float(P),
                                    base=-E, pattern=[[0, 1]], channel_multiplier=1).then_inc(s_const, 1)
            nc.gpsimd.iota(ecol[:, 2:3], pattern=[[0, 1]], base=0, channel_multiplier=1,
                           allow_small_or_imprecise_dtypes=True).then_inc(s_const, 1)
            nc.gpsimd.affine_select(out=ecol[:, 3:4], in_=ecol[:, 3:4], compare_op=ALU.is_gt, fill=float(NB),
                                    base=E, pattern=[[0, 1]], channel_multiplier=-1).then_inc(s_const, 1)
            pool.wait_ge(s_const, 18)
            nc.gpsimd.affine_select(out=ecol[:, 2:3], in_=ecol[:, 2:3], compare_op=ALU.is_gt, fill=0.0,
                                    base=E, pattern=[[0, 1]], channel_multiplier=-1).then_inc(s_const, 1)
            nc.gpsimd.iota(yrow[:, :, H].bitcast(I32), pattern=[[P, NT]], base=0,
                           channel_multiplier=1).then_inc(s_dest, 1)

            def scatter(g, k, done):
                for t in range(g * GT, (g + 1) * GT):
                    nc.gpsimd.indirect_dma_start(
                        out=xs, out_offset=bass.IndirectOffsetOnAxis(ap=slot[:, t, k:k + 1], axis=0),
                        in_=yrow[:, t, :], in_offset=None).then_inc(done, 16)

            def second_choices(g):
                pool.wait_ge(s_first[g], 16 * GT)
                dest = yrow[:, g * GT:(g + 1) * GT, H].bitcast(I32)
                nc.gpsimd.tensor_scalar(dest, dest, float(T), None, ALU.add).then_inc(s_dest, 1)
                pool.wait_ge(s_dest, g + 2)
                scatter(g, 1, s_second)

            def first_choices(g):
                pool.wait_ge(s_slot, g + 1)
                pool.wait_ge(s_yn, 2 * (g + 1))
                scatter(g, 0, s_first[g])

            pool.wait_ge(s_dest, 1)
            first_choices(0)
            second_choices(0)
            first_choices(1)
            for g in range(1, NG - 1):
                first_choices(g + 1)
                second_choices(g)
            second_choices(NG - 1)

            last_row = pool.to_reg(T * TOPK - 1)
            pairs_wanted = pool.alloc_register("pairs_wanted")
            pool.reg_mov(pairs_wanted, 0)

            def store_blocks():
                for s in range(RING):
                    if s % 2 == 0:
                        pool.reg_add(pairs_wanted, pairs_wanted, 1)
                    pool.wait_ge(s_dest, NG + 1)
                    pool.wait_ge(s_res, pairs_wanted)
                    nc.gpsimd.indirect_dma_start(
                        out=rs, out_offset=bass.IndirectOffsetOnAxis(ap=idx[:, s:s + 1], axis=0),
                        in_=res[:, s, :], in_offset=None,
                        bounds_check=last_row, oob_is_err=False).then_inc(s_stored[s // 2], 16)

            with pool.Fori(0, ITERS):
                store_blocks()

        @block.scalar
        def _(act_e):
            act_e.dma_start(fcb[:, :], fc_bias.rearrange("(c p) -> p c", p=P),
                            allow_slow_non_contiguous=True).then_inc(s_bias_in, 16)
            for b in range(B):
                act_e.dma_start(cnd[:, b, :], cond[b, :].rearrange("(c p) -> p c", p=P),
                                allow_slow_non_contiguous=True).then_inc(s_bias_in, 16)
            act_e.dma_start(rw[:, :, :], router_w.rearrange("(c p) e -> p c e", p=P)).then_inc(s_router_in, 16)
            act_e.preload_act_table(ACT.Gelu)

            act_e.wait_ge(s_fsT_ps, 1)
            nc.scalar.activation(fsT[:, :, :], bank[4][0:R, :].rearrange("r (b h) -> r b h", b=B),
                                 ACT.Copy).then_inc(s_fsT, 1)
            act_e.wait_ge(s_wT_ps, 1)
            nc.scalar.activation(wT[:, :, :], bank[5][:, :].rearrange("p (c h) -> p c h", c=HC),
                                 ACT.Copy).then_inc(s_wT, 1)

            act_e.wait_ge(s_cbias, 1)
            for g in range(NG):
                for oc in range(HC):
                    act_e.wait_ge(s_cond, g * HC + oc + 1)
                    if g >= 2 and oc == 0:
                        act_e.wait_ge(s_yn_ps, 2 * (g - 1))
                    nc.scalar.activation(yT[:, g % 2, oc, :], cond_ps[oc][:, :], ACT.Gelu,
                                         bias=cbias[:, g // GPB, oc:oc + 1]).then_inc(s_yT, 1)
                for h in range(2):
                    act_e.wait_ge(s_yn_ps, 2 * g + h + 1)
                    t = g * GT + 2 * h
                    nc.scalar.activation(yrow[:, t:t + 2, 0:H], yn_ps[h], ACT.Copy).then_inc(s_yn, 1)
                for e in SPLIT_AFTER[g]:
                    act_e.wait_ge(s_w[e // WE], 32)
                    gu, dn = slice(e * HC * F2, (e + WE) * HC * F2), slice(e * H, (e + WE) * H)
                    nc.scalar.activation(wgu["hi"][:, gu], wgu_raw[:, gu], ACT.Copy).then_inc(s_whi, 1)
                    nc.scalar.activation(wd["hi"][:, dn], wd_raw[:, dn], ACT.Copy).then_inc(s_whi, 1)
            act_e.wait_ge(s_ldif, 1)
            nc.scalar.activation(score[:, 0, :], ldif[:, :], ACT.Sigmoid).then_inc(s_score, 1)
            nc.scalar.activation(score[:, 1, :], ldif[:, :], ACT.Sigmoid, scale=-1.0).then_inc(s_score, 1)

            def y_hi(p, u):
                act_e.wait_ge(s_ygT_ps, p + 1)
                need(act_e, s_gu, p - 1)
                nc.scalar.activation(ygT["hi"][:, u % 2], ygT_ps[u % 2], ACT.Copy).then_inc(s_yhi, 1)

            def act_hi(p, u):
                act_e.wait_ge(s_actT_ps, p + 1)
                need(act_e, s_dn, p - 1)
                nc.scalar.activation(actT["hi"][:, u % 2], actT_ps[u % 2], ACT.Copy).then_inc(s_ahi, 1)

            def sigmoid(p, u):
                act_e.wait_ge(s_gu, p + 1)
                need(act_e, s_act, p - 1)
                nc.scalar.activation(sig[:, u % 2], gu_ps[u % 2][:, :, 0:F2:2], ACT.Sigmoid,
                                     scale=ALPHA).then_inc(s_sig, 1)

            def copy_res(i, u):
                act_e.wait_ge(s_dn, i * PAIRS_IN_BODY + u + 1)
                nc.scalar.activation(res[:, 2 * u:2 * u + 2, :], dn_ps[u % 2], ACT.Copy).then_inc(s_res, 1)

            def copy_index(i, u):
                need(act_e, s_stored[u], 32 * i)
                nc.scalar.copy(idx[:, 2 * u:2 * u + 2], yg[:, 2 * u:2 * u + 2, H].bitcast(U32)).then_inc(s_idx, 1)

            def experts(i, first=False, last=False):
                for u in range(PAIRS_IN_BODY):
                    p = i * PAIRS_IN_BODY + u
                    if not (last and u == PAIRS_IN_BODY - 1):
                        y_hi(p + 1, u + 1)
                    sigmoid(p, u)
                    if not (first and u == 0):
                        act_hi(p - 1, u - 1)
                    copy_index(i, u)
                    if not (first and u <= 1):
                        copy_res(*earlier(i, u, 2))

            y_hi(0, 0)
            experts(0, first=True)
            with act_e.Fori(1, ITERS - 1) as i:
                experts(i)
            experts(ITERS - 1, last=True)
            act_hi(ITERS * PAIRS_IN_BODY - 1, PAIRS_IN_BODY - 1)
            copy_res(ITERS - 1, PAIRS_IN_BODY - 2)
            copy_res(ITERS - 1, PAIRS_IN_BODY - 1)

            for t in range(0, NT, 2):
                act_e.wait_ge(s_sum, t + 2)
                act_e.dma_start(out_v[:, t:t + 2, :], x_sb[:, t:t + 2, :]).then_inc(s_out, 16)
            act_e.wait_ge(s_out, 16 * NT // 2)

        @block.tensor
        def _(pe):
            def warm_up(n, spare):
                for _ in range(n):
                    nc.tensor.transpose(spare[:, 0:P], ident[:, :], ident[:, :])

            pe.wait_ge(s_ident, 1)
            warm_up(WARM0, bank[3])
            pe.wait_ge(s_in, 32)
            for b in range(B):
                for c in range(HC):
                    last = nc.tensor.matmul(bank[4][0:R, (b * HC + c) * P:(b * HC + c + 1) * P],
                                            fs_nat[:, b, c, :], ident[:, :], start=True, stop=True)
            last.then_inc(s_fsT_ps, 1)
            for ic in range(HC):
                for oc in range(HC):
                    last = nc.tensor.transpose(bank[5][:, ic * H + oc * P:ic * H + (oc + 1) * P],
                                               w_nat[:, oc, ic * P:(ic + 1) * P], ident[:, :])
            last.then_inc(s_wT_ps, 1)
            def side_product(b):
                pe.wait_ge(s_fsT, 2)
                for ic in range(HC):
                    last = nc.tensor.matmul(bank[6 + b][:, ic * H:(ic + 1) * H], fsTs[:, b, ic * P:(ic + 1) * P],
                                            fsT[:, b, :], start=True, stop=True)
                last.then_inc(s_side_ps, 1)

            def transpose_x(g):
                pe.wait_ge(s_x[g], 16)
                for c in range(HC):
                    if g >= 1:
                        pe.wait_ge(s_xT, (g - 1) * HC + c + 1)
                    for q in range(GT):
                        last = nc.tensor.transpose(xT_ps[c][:, q * P:(q + 1) * P],
                                                   x_sb[:, g * GT + q, c * P:(c + 1) * P], ident[:, :])
                    last.then_inc(s_xT_ps, 1)

            def cond_product(g):
                pe.wait_ge(s_xT, (g + 1) * HC)
                for oc in range(HC):
                    if g >= 1:
                        pe.wait_ge(s_yT, (g - 1) * HC + oc + 1)
                    for ic in range(HC):
                        last = nc.tensor.matmul(cond_ps[oc][:, :], weff[:, g // GPB, ic, oc * P:(oc + 1) * P],
                                                xT[:, g % 2, ic, :], start=(ic == 0), stop=(ic == HC - 1))
                    last.then_inc(s_cond, 1)

            def logits(g):
                pe.wait_ge(s_yT, (g + 1) * HC)
                if g >= 1:
                    pe.wait_ge(s_lg, g)
                for q in range(GT):
                    for c in range(HC):
                        last = nc.tensor.matmul(lg_ps[:, q, :], yT[:, g % 2, c, q * P:(q + 1) * P], rw[:, c, :],
                                                start=(c == 0), stop=(c == HC - 1))
                last.then_inc(s_lg_ps, 1)

            def y_by_token(g):
                for h in range(2):
                    if g >= 1:
                        pe.wait_ge(s_yn, 2 * (g - 1) + h + 1)
                    for j in range(2):
                        q = 2 * h + j
                        for c in range(HC):
                            last = nc.tensor.transpose(yn_ps[h][:, j, c * P:(c + 1) * P],
                                                       yT[:, g % 2, c, q * P:(q + 1) * P], ident[:, :])
                    last.then_inc(s_yn_ps, 1)

            def ranks(g):
                pe.wait_ge(s_gsum, g + 1)
                if g >= 1:
                    pe.wait_ge(s_slot, g)
                nc.tensor.matmul(rank_ps, tri[:, :], multi[:, :, 0:E], start=True, stop=False)
                for q in range(GT - 1):
                    n = GT - 1 - q
                    last = nc.tensor.matmul(rank_ps[:, q + 1:GT, :], ones_b[:, :],
                                            multi[:, q:q + 1, 0:E].broadcast_to([P, n, E]),
                                            start=False, stop=(g == 0 and q == GT - 2))
                for j in range(g):
                    last = nc.tensor.matmul(rank_ps, ones_b[:, :], gsum[:, j:j + 1, 0:E].broadcast_to([P, GT, E]),
                                            start=False, stop=(j == g - 1))
                last.then_inc(s_rank, 1)

            transpose_x(0)
            side_product(0)
            side_product(1)
            pe.wait_ge(s_weff, 1)
            cond_product(0)
            transpose_x(1)
            pe.wait_ge(s_router_in, 16)
            pe.wait_ge(s_weff, B)
            pe.wait_ge(s_const, 19)
            for g in range(NG):
                logits(g)
                y_by_token(g)
                if g != 1:
                    ranks(g)
                if g + 1 < NG:
                    cond_product(g + 1)
                if g == 1:
                    ranks(g)
                if g + 2 < NG:
                    transpose_x(g + 2)

            pe.wait_ge(s_slot, NG)
            for g in range(NG):
                last = nc.tensor.matmul(bank[5][0:E1, 128:129], gsum[:, g, :], ones_b[:, 0:1],
                                        start=(g == 0), stop=(g == NG - 1))
            last.then_inc(s_cnt, 1)
            pe.wait_ge(s_nblk, 1)
            nc.tensor.matmul(bank[5][0:E1, 136:137], trif[:, :], nblk[:, :], start=True, stop=True).then_inc(s_pre, 1)
            pe.wait_ge(s_own, 1)
            nc.tensor.matmul(bank[5][0:1, 144:144 + NB], ones_f[:, 0:1], rowown[:, :], start=True, stop=True)
            nc.tensor.matmul(bank[5][0:1, 208:208 + NB], ecol[:, 2:3], owner[:, :],
                             start=True, stop=True).then_inc(s_tab_ps, 1)

            pe.wait_ge(s_table, 1)
            warm_up(WARM1, bank[4])
            pe.wait_ge(s_wlo, E // WE)
            pe.wait_ge(s_brow, 64)
            pe.wait_ge(s_picks, 1)
            pe.wait_ge(s_yn, 2 * NG)

            TERMS = (("hi", "hi"), ("hi", "lo"), ("lo", "hi"))

            def transpose_y(i, u):
                pe.wait_ge(s_yg[u], 32 * i + 32)
                for j in range(2):
                    for c in range(HC):
                        last = nc.tensor.transpose(ygT_ps[u % 2][:, j, c, :], yg[:, 2 * u + j, c * P:(c + 1) * P],
                                                   ident[:, :])
                last.then_inc(s_ygT_ps, 1)

            def gate_up_product(i, u, owners):
                pe.wait_ge(s_ylo, i * PAIRS_IN_BODY + u + 1)
                for j in range(2):
                    e = owners[j]
                    o = gu_ps[u % 2][:, j, :]
                    for c in range(HC):
                        for n, (yp, wp) in enumerate(TERMS):
                            nc.tensor.matmul(o, ygT[yp][:, u % 2, j, c, :],
                                             wgu[wp][:, bass.ds(e * (HC * F2) + c * F2, F2)],
                                             start=(c == 0 and n == 0), stop=False)
                    last = nc.tensor.matmul(o, picks[:, 0, :], brow[:, bass.ds(e * F2, F2)], start=False, stop=True)
                last.then_inc(s_gu, 1)

            def transpose_act(i, u):
                pe.wait_ge(s_act, i * PAIRS_IN_BODY + u + 1)
                for j in range(2):
                    last = nc.tensor.transpose(actT_ps[u % 2][:, j, :], act[:, u % 2, j, :], ident[:, :])
                last.then_inc(s_actT_ps, 1)

            def down_product(i, u, owners):
                p = i * PAIRS_IN_BODY + u
                pe.wait_ge(s_alo, p + 1)
                need(pe, s_res, p - 1)
                for j in range(2):
                    e = owners[j]
                    o = dn_ps[u % 2][:, j, :]
                    for n, (ap, wp) in enumerate(TERMS):
                        nc.tensor.matmul(o, actT[ap][:, u % 2, j, :], wd[wp][:, bass.ds(e * H, H)],
                                         start=(n == 0), stop=False)
                    last = nc.tensor.matmul(o, picks[:, 1, :], brow[:, bass.ds(e * H, H)], start=False, stop=True)
                last.then_inc(s_dn, 1)

            def experts(i, first=False, last=False):
                end = PAIRS_IN_BODY - 1
                back = 0 if first else 4
                owners = table_values(mybir.EngineType.PE, 1, i * RING - back, RING + back, E - 1)
                for u in range(PAIRS_IN_BODY):
                    if u < end:
                        transpose_y(i, u + 1)
                    elif not last:
                        transpose_y(i + 1, 0)
                    at = back + 2 * u
                    gate_up_product(i, u, owners[at:at + 2])
                    if not (first and u == 0):
                        transpose_act(*earlier(i, u, 1))
                    if not (first and u <= 1):
                        down_product(*earlier(i, u, 2), owners[at - 4:at - 2])

            transpose_y(0, 0)
            experts(0, first=True)
            with pe.Fori(1, ITERS - 1) as i:
                experts(i)
            experts(ITERS - 1, last=True)
            owners = table_values(mybir.EngineType.PE, 1, NB - 4, 4, E - 1)
            transpose_act(ITERS - 1, PAIRS_IN_BODY - 1)
            down_product(ITERS - 1, PAIRS_IN_BODY - 2, owners[0:2])
            down_product(ITERS - 1, PAIRS_IN_BODY - 1, owners[2:4])

        @block.vector
        def _(dve):
            own_steps = [0]

            def after(ins):
                own_steps[0] += 1
                ins.then_inc(s_v, 1)
                dve.wait_ge(s_v, own_steps[0])

            dve.wait_ge(s_fsT, 1)
            nc.vector.tensor_scalar(fsTs[:, :, :], fsT[:, :, :], 1.0 / (H * R), None, ALU.mult).then_inc(s_fsT, 1)
            dve.wait_ge(s_bias_in, 16 * (1 + B))
            for b in range(B):
                last = nc.vector.tensor_tensor(cbias[:, b, :], cnd[:, b, :], fcb[:, :], ALU.add)
            last.then_inc(s_cbias, 1)

            def add_side(b):
                dve.wait_ge(s_side_ps, b + 1)
                dve.wait_ge(s_wT, 1)
                nc.vector.tensor_tensor(weff[:, b, :, :], bank[6 + b][:, :].rearrange("p (c h) -> p c h", c=HC),
                                        wT[:, :, :], ALU.add).then_inc(s_weff, 1)

            def split_biases():
                dve.wait_ge(s_eb, 32)
                ups = braw[:, 0, 1:F2:2]
                after(nc.vector.tensor_scalar(ups, ups, 1.0, None, ALU.add))
                nc.vector.tensor_copy(bsplit["hi"][:, :, :], braw[:, :, :]).then_inc(s_bsplit, 1)
                dve.wait_ge(s_bsplit, 1)
                nc.vector.tensor_tensor(bsplit["lo"][:, :, :], braw[:, :, :], bsplit["hi"][:, :, :].bitcast(FP32),
                                        ALU.subtract).then_inc(s_bsplit, 1)
                nc.vector.tensor_copy(picks[:, :, :], picksf[:, :, :]).then_inc(s_picks, 1)

            def split_weights(g):
                for e in SPLIT_AFTER[g]:
                    dve.wait_ge(s_whi, 2 * (e // WE + 1))
                    gu, dn = slice(e * HC * F2, (e + WE) * HC * F2), slice(e * H, (e + WE) * H)
                    nc.vector.tensor_tensor(wgu["lo"][:, gu], wgu_raw[:, gu], wgu["hi"][:, gu].bitcast(FP32),
                                            ALU.subtract)
                    nc.vector.tensor_tensor(wd["lo"][:, dn], wd_raw[:, dn], wd["hi"][:, dn].bitcast(FP32),
                                            ALU.subtract).then_inc(s_wlo, 1)

            def copy_xT(g):
                for c in range(HC):
                    dve.wait_ge(s_xT_ps, g * HC + c + 1)
                    if g >= 2:
                        dve.wait_ge(s_cond, (g - 1) * HC)
                    nc.vector.tensor_copy(xT[:, g % 2, c, :], xT_ps[c][:, :]).then_inc(s_xT, 1)

            def choose(g):
                ts = slice(g * GT, (g + 1) * GT)
                dve.wait_ge(s_lg_ps, g + 1)
                nc.vector.tensor_copy(lg[:, ts, :], lg_ps).then_inc(s_lg, 1)
                dve.wait_ge(s_lg, g + 1)
                for t in range(g * GT, (g + 1) * GT):
                    last = nc.vector.max(top[:, t, :], lg[:, t, :])
                after(last)
                for t in range(g * GT, (g + 1) * GT):
                    last = nc.vector.max_index(topi[:, t, :], top[:, t, :], lg[:, t, :])
                after(last)
                if g >= 1:
                    dve.wait_ge(s_rank, g)
                after(nc.vector.tensor_tensor(
                    mask[:, :, :, :], topi[:, ts, 0:TOPK].unsqueeze(3).broadcast_to([P, GT, TOPK, E]),
                    iota_e[:, :].unsqueeze(1).unsqueeze(1).broadcast_to([P, GT, TOPK, E]), ALU.is_equal))
                after(nc.vector.tensor_tensor(multi[:, :, 0:E], mask[:, :, 0, :], mask[:, :, 1, :], ALU.add))
                with nc.allow_low_precision("counts up to 8 are exact"):
                    nc.vector.tensor_reduce(gsum[:, g, :], multi[:, :, :].rearrange("p t e -> p e t"),
                                            axis=AX.X, op=ALU.add).then_inc(s_gsum, 1)

            def place(g):
                ts = slice(g * GT, (g + 1) * GT)
                dve.wait_ge(s_rank, g + 1)
                after(nc.vector.tensor_tensor(rbase[:, :, :], rank_ps,
                                              ebase[:, :].unsqueeze(1).broadcast_to([P, GT, E]), ALU.add))
                after(nc.vector.tensor_tensor(prod[:, :, :, :], mask[:, :, :, :],
                                              rbase[:, :, :].unsqueeze(2).broadcast_to([P, GT, TOPK, E]), ALU.mult))
                with nc.allow_low_precision("row numbers are integers below 2^24"):
                    nc.vector.tensor_reduce(slot[:, ts, :], prod[:, :, :, :], axis=AX.X, op=ALU.add).then_inc(s_slot, 1)

            copy_xT(0)
            add_side(0)
            add_side(1)
            dve.wait_ge(s_const, 19)
            nc.vector.memset(multi[:, :, :], 0.0).then_inc(s_dv, 1)
            dve.wait_ge(s_dv, 1)
            copy_xT(1)
            for g in range(NG):
                choose(g)
                if g == 1:
                    split_weights(g)
                place(g)
                if g == 0:
                    split_biases()
                if g + 2 < NG:
                    copy_xT(g + 2)
                if g == 2:
                    split_weights(g)
            nc.vector.tensor_tensor(ldif[:, :], top[:, :, 0], top[:, :, 1], ALU.subtract).then_inc(s_ldif, 1)

            dve.wait_ge(s_cnt, 1)
            after(nc.vector.tensor_copy(cnt[:, :], bank[5][0:E1, 128:129]))
            after(nc.vector.tensor_scalar(over[:, :], iota_cnt[:, :], cnt[:, 0:1], None, ALU.is_lt))
            after(nc.vector.tensor_reduce(nblk[:, :], over[:, :], axis=AX.X, op=ALU.add))
            nc.vector.tensor_tensor(nblk[:, :], nblk[:, :], ecol[:, 3:4], ALU.add).then_inc(s_nblk, 1)
            dve.wait_ge(s_pre, 1)
            after(nc.vector.tensor_copy(cexc[:, :], bank[5][0:E1, 136:137]))
            after(nc.vector.tensor_tensor(cinc[:, :], cexc[:, :], nblk[:, :], ALU.add))
            after(nc.vector.tensor_tensor(base[:, :], cexc[:, :], ecol[:, 1:2], ALU.mult))
            after(nc.vector.tensor_tensor(base[:, :], base[:, :], cnt[:, :], ALU.add))
            after(nc.vector.tensor_tensor(base[:, :], base[:, :], ecol[:, 0:1], ALU.add))
            after(nc.vector.tensor_scalar(started[:, :], iota_blk[:, :], cexc[:, 0:1], None, ALU.is_ge))
            after(nc.vector.scalar_tensor_tensor(owner[:, :], iota_blk[:, :], cinc[:, 0:1], started[:, :],
                                                 ALU.is_lt, ALU.mult))
            after(nc.vector.tensor_scalar(rowat[:, :], iota_blk[:, :], ecol[:, 1:2], base[:, 0:1],
                                          ALU.mult, ALU.subtract))
            nc.vector.scalar_tensor_tensor(rowown[:, :], rowat[:, :], -1.0, owner[:, :],
                                           ALU.mult, ALU.mult).then_inc(s_own, 1)
            dve.wait_ge(s_tab_ps, 1)
            after(nc.vector.tensor_copy(table[0:1, 0, :], bank[5][0:1, 144:144 + NB]))
            nc.vector.tensor_copy(table[0:1, 1, :], bank[5][0:1, 208:208 + NB]).then_inc(s_table, 1)

            split_weights(NG - 1)

            def y_lo(p, u):
                dve.wait_ge(s_yhi, p + 1)
                nc.vector.tensor_tensor(ygT["lo"][:, u % 2], ygT_ps[u % 2], ygT["hi"][:, u % 2].bitcast(FP32),
                                        ALU.subtract).then_inc(s_ylo, 1)

            def act_lo(p, u):
                dve.wait_ge(s_ahi, p + 1)
                nc.vector.tensor_tensor(actT["lo"][:, u % 2], actT_ps[u % 2], actT["hi"][:, u % 2].bitcast(FP32),
                                        ALU.subtract).then_inc(s_alo, 1)

            def activate(p, u):
                b = u % 2
                dve.wait_ge(s_sig, p + 1)
                nc.vector.tensor_scalar(up1[:, b], gu_ps[b][:, :, 1:F2:2], 1.0 - LIMIT, 1.0 + LIMIT,
                                        ALU.max, ALU.min).then_inc(s_dv, 1)
                dve.wait_ge(s_dv, 2 * p + 2)
                need(dve, s_actT_ps, p - 1)
                nc.vector.scalar_tensor_tensor(gup[:, b], gu_ps[b][:, :, 0:F2:2], LIMIT, up1[:, b],
                                               ALU.min, ALU.mult).then_inc(s_dv, 1)
                dve.wait_ge(s_dv, 2 * p + 3)
                nc.vector.scalar_tensor_tensor(act[:, b], sig[:, b], SIG_MAX, gup[:, b],
                                               ALU.min, ALU.mult).then_inc(s_act, 1)

            def experts(i, first=False, last=False):
                for u in range(PAIRS_IN_BODY):
                    p = i * PAIRS_IN_BODY + u
                    if not (last and u == PAIRS_IN_BODY - 1):
                        y_lo(p + 1, u + 1)
                    activate(p, u)
                    if not (first and u == 0):
                        act_lo(p - 1, u - 1)

            y_lo(0, 0)
            experts(0, first=True)
            with dve.Fori(1, ITERS - 1) as i:
                experts(i)
            experts(ITERS - 1, last=True)
            act_lo(ITERS * PAIRS_IN_BODY - 1, PAIRS_IN_BODY - 1)

            dve.wait_ge(s_score, 2)
            for g in range(NG):
                dve.wait_ge(s_back[g], 16 * TOPK)
                for k in range(TOPK):
                    for t in range(g * GT, (g + 1) * GT):
                        r = second(t) if k else yrow[:, t, 0:H]
                        last = nc.vector.scalar_tensor_tensor(x_sb[:, t, :], r, score[:, k, t:t + 1],
                                                              x_sb[:, t, :], ALU.mult, ALU.add)
                        if k == TOPK - 1:
                            last.then_inc(s_sum, 1)
                    if k == 0:
                        last.then_inc(s_part, 1)
                        dve.wait_ge(s_part, g + 1)


_INS = ["x", "fside_Bx1x1024x16_0", "cond_1024", "L0_cond_W", "L0_cond_fc_bias", "L0_ffn_router_weight",
        "L0_ffn_gate_up_proj", "L0_ffn_gate_up_proj_bias", "L0_ffn_down_proj", "L0_ffn_down_proj_bias"]


def kernel(**inputs):
    import numpy as np
    import concourse.bacc as bacc
    from concourse.bass_utils import run_bass_kernel_spmd

    nc = bacc.Bacc("TRN2", target_bir_lowering=False, num_devices=1)
    arrays, args = {}, []
    for name in _INS:
        a = np.ascontiguousarray(inputs[name])
        arrays[f"in_{name}"] = a
        args.append(nc.dram_tensor(f"in_{name}", a.shape, mybir.dt.from_np(a.dtype), kind="ExternalInput").ap())
    shape = inputs["x"].shape
    out = nc.dram_tensor("out", shape, FP32, kind="ExternalOutput").ap()
    adaln_moe_ffn(nc, *args, out)
    r = run_bass_kernel_spmd(nc, [arrays], core_ids=[0])
    return r.results[0]["out"]
```

```python
import math

import concourse.bass as bass
from concourse import mybir
from contextlib import ExitStack

FP32 = mybir.dt.float32
FP32R = mybir.dt.float32r
BF16 = mybir.dt.bfloat16
U32 = mybir.dt.uint32
I32 = mybir.dt.int32
ALU = mybir.AluOpType
ACT = mybir.ActivationFunctionType
AX = mybir.AxisListType

ALPHA, LIMIT = 1.702, 7.0
GLU_MAX = LIMIT / (1.0 + math.exp(-ALPHA * LIMIT))


def adaln_moe_ffn(nc, x, fside, cond, cond_w, fc_bias, router_w, gate_up, gate_up_bias, down, down_bias, out):
    P = 128
    B, S, H = x.shape
    R = fside.shape[3]
    E, _, F2 = gate_up.shape
    INTER = F2 // 2
    TOPK = 2
    T = B * S
    NT = T // P
    HC = H // P
    GT = 4
    NG = NT // GT
    GPB = NG // B
    MAX_BLOCKS = T * TOPK // P + E - 1
    PAIRS_IN_BODY = 4
    RING = 2 * PAIRS_IN_BODY
    ITERS = -(-MAX_BLOCKS // RING)
    NB = ITERS * RING
    REGION = T + P
    XROWS = E * REGION + P
    WE = 2
    WARM_START, WARM_W, WARM_GAP, WARM_BIAS, WARM_SPREAD, WARM_EXPERTS = 11, 4, 10, 16, 2, 4
    PARTS = ("hi", "lo")
    SPLIT_AT = (0, WE, 3 * WE, 5 * WE, E)
    SPLIT_AFTER = [range(SPLIT_AT[g], SPLIT_AT[g + 1], WE) for g in range(NG)]
    RW = H + 1
    SKIP = T * TOPK
    E1 = E + 1

    x_v = x.rearrange("b (t p) h -> p (b t) h", p=P)
    out_v = out.rearrange("b (t p) h -> p (b t) h", p=P)
    xs = nc.dram_tensor("dispatched", (XROWS, RW), FP32, kind="Internal").ap()
    rs = nc.dram_tensor("pair_results", (T * TOPK, H), FP32, kind="Internal").ap()
    rs_v = rs.rearrange("(k t p) h -> p k t h", p=P, k=TOPK)

    ctx = ExitStack()
    with ctx:
        def sb(name, shape, dt=FP32):
            return ctx.enter_context(nc.sbuf_tensor(name, shape, dt))

        def sem(name):
            return ctx.enter_context(nc.semaphore(name))

        x_sb = sb("x_sb", [P, NT, H])
        fs_nat = sb("fs_nat", [P, B, HC, R])
        fcb = sb("fcb", [P, HC])
        cnd = sb("cnd", [P, B, HC])
        rw = sb("rw", [P, HC, E])
        wgu_raw = sb("wgu_raw", [P, E * HC * F2])
        wd_raw = sb("wd_raw", [P, E * H])
        wgu = {"hi": sb("wgu_hi", [P, E * HC * F2], FP32R), "lo": wgu_raw[:, :].bitcast(FP32R)}
        wd = {"hi": sb("wd_hi", [P, E * H], FP32R), "lo": wd_raw[:, :].bitcast(FP32R)}
        braw = sb("braw", [E, 2, F2])
        bsplit = {part: sb(f"bsplit_{part}", [E, 2, F2], FP32R) for part in PARTS}
        gub2 = sb("gub2", [2 * E, F2], FP32R)
        sel = sb("sel", [2 * E, E], FP32R)
        db3 = sb("db3", [3 * E, H], FP32R)
        gu_bias = sb("gu_bias", [P, E * F2])
        ident = sb("ident", [P, P])
        tri = sb("tri", [P, P], BF16)
        trif = sb("trif", [E1, E1])
        ones_b = sb("ones_b", [P, P], BF16)
        ones_f = sb("ones_f", [E1, P])
        iota_e = sb("iota_e", [P, E])
        ebase = sb("ebase", [P, E])
        iota_blk = sb("iota_blk", [E1, NB])
        iota_cnt = sb("iota_cnt", [E1, NT])
        ecol = sb("ecol", [E1, 4])
        pad = sb("pad", [P, RW])
        room = sb("room", [P, 3, 2 * 2 * INTER])
        w_nat = room[:, 0, :].rearrange("p (c i) -> p c i", c=HC)
        fsT = room[0:R, 1, :].rearrange("r (b h) -> r b h", b=B)
        fsTs = room[0:R, 2, :].rearrange("r (b h) -> r b h", b=B)
        wT = sb("wT", [P, HC, H])
        weff = sb("weff", [P, B, HC, H])
        cbias = sb("cbias", [P, B, HC])
        yrow = sb("yrow", [P, NT, RW])
        lg = sb("lg", [P, NT, E])
        top = sb("top", [P, NT, 8])
        topi = sb("topi", [P, NT, 8], U32)
        mask = sb("mask", [P, GT, TOPK, E])
        multi = sb("multi", [P, GT, E1], BF16)
        gsum = sb("gsum", [P, NG, E1], BF16)
        rbase = sb("rbase", [P, GT, E])
        prod = sb("prod", [P, GT, TOPK, E])
        slot = sb("slot", [P, NT, TOPK], U32)
        ldif = sb("ldif", [P, NT])
        score = sb("score", [P, TOPK, NT])
        chosen = wT[:, :, :].rearrange("p c h -> p (c h)")[:, 0:NT * TOPK * E].rearrange(
            "p (t k e) -> p t k e", t=NT, k=TOPK)
        weff_room = weff[:, :, :, :].rearrange("p b c h -> p (b c h)")
        dense = weff_room[:, 0:NT * E].rearrange("p (t e) -> p t e", t=NT)
        dense3 = weff_room[:, NT * E:4 * NT * E].rearrange("p (t n e) -> p t n e", t=NT, n=3)
        cnt = sb("cnt", [E1, 1])
        over = sb("over", [E1, NT])
        nblk = sb("nblk", [E1, 1])
        cexc = sb("cexc", [E1, 1])
        cinc = sb("cinc", [E1, 1])
        base = sb("base", [E1, 1])
        started = sb("started", [E1, NB])
        owner = sb("owner", [E1, NB])
        rowat = sb("rowat", [E1, NB])
        rowown = sb("rowown", [E1, NB])
        table = sb("table", [1, 2, NB], I32)
        yg = sb("yg", [P, RING, RW])
        idx = sb("idx", [P, RING], U32)
        ygT = {part: sb(f"ygT_{part}", [P, 2, 2, HC, P], FP32R) for part in PARTS}
        glu, up1, act = (room[:, n, :].rearrange("p (b j f) -> p b j f", b=2, j=2) for n in range(3))
        gub = sb("gub", [P, 2, 2, F2])
        actT = {part: sb(f"actT_{part}", [P, 2, 2, P], FP32R) for part in PARTS}
        res = sb("res", [P, RING, H])
        xT = yg[:, :, :].rearrange("p a b -> p (a b)")[:, 0:2 * HC * GT * P].rearrange(
            "p (b c s) -> p b c s", b=2, c=HC)
        scoreT = [ygT[part][0:3 * E].rearrange("e a b c s -> e (a b c s)") for part in PARTS]
        yT = res[:, :, :].rearrange("p a b -> p (a b)").rearrange("p (b c s) -> p b c s", b=2, c=HC)
        def second(t):
            return yg[:, t, 0:H] if t < RING else res[:, t - RING, :]

        bank = [ctx.enter_context(nc.psum_tensor(f"bank{i}", [P, 512], FP32)) for i in range(8)]

        s_ident0 = sem("s_ident0")
        s_ident = sem("s_ident")
        s_const = sem("s_const")
        s_pad = sem("s_pad")
        s_dest = sem("s_dest")
        s_side_in = sem("s_side_in")
        s_w_in = sem("s_w_in")
        s_bias_in = sem("s_bias_in")
        s_router_in = sem("s_router_in")
        s_x = [sem(f"s_x{g}") for g in range(NG)]
        s_w = [sem(f"s_w{n}") for n in range(E // WE)]
        s_whi = sem("s_whi")
        s_wlo = sem("s_wlo")
        s_bsplit = sem("s_bsplit")
        s_db3 = sem("s_db3")
        s_ups = sem("s_ups")
        s_gub2 = sem("s_gub2")
        s_sel = sem("s_sel")
        s_gu_bias_ps = sem("s_gu_bias_ps")
        s_gu_bias = sem("s_gu_bias")
        s_gub = sem("s_gub")
        s_wT_ps = sem("s_wT_ps")
        s_wT = sem("s_wT")
        s_side_ps = sem("s_side_ps")
        s_eb = sem("s_eb")
        s_prefill = sem("s_prefill")
        s_fsT_ps = sem("s_fsT_ps")
        s_fsT = sem("s_fsT")
        s_weff = sem("s_weff")
        s_cbias = sem("s_cbias")
        s_xT_ps = sem("s_xT_ps")
        s_xT = sem("s_xT")
        s_xT_act = sem("s_xT_act")
        s_cond = sem("s_cond")
        s_yT = sem("s_yT")
        s_lg_ps = sem("s_lg_ps")
        s_lg = sem("s_lg")
        s_yn_ps = sem("s_yn_ps")
        s_yn = sem("s_yn")
        s_gsum = sem("s_gsum")
        s_multi = sem("s_multi")
        s_rank = sem("s_rank")
        s_slot = sem("s_slot")
        s_v = sem("s_v")
        s_first = [[sem(f"s_first{g}_{h}") for h in range(2)] for g in range(NG)]
        s_second = sem("s_second")
        s_cnt = sem("s_cnt")
        s_nblk = sem("s_nblk")
        s_pre = sem("s_pre")
        s_own = sem("s_own")
        s_tab_ps = sem("s_tab_ps")
        s_table = sem("s_table")
        s_yg = [sem(f"s_yg{u}") for u in range(PAIRS_IN_BODY)]
        s_ygT_ps = sem("s_ygT_ps")
        s_yhi = sem("s_yhi")
        s_ylo = sem("s_ylo")
        s_gu = sem("s_gu")
        s_glu = sem("s_glu")
        s_act = sem("s_act")
        s_actT_ps = sem("s_actT_ps")
        s_ahi = sem("s_ahi")
        s_alo = sem("s_alo")
        s_dn = sem("s_dn")
        s_res = sem("s_res")
        s_stored = [sem(f"s_stored{u}") for u in range(PAIRS_IN_BODY)]
        s_idx = sem("s_idx")
        s_up1 = sem("s_up1")
        s_back = [[sem(f"s_back{k}_{g}") for g in range(NG)] for k in range(TOPK)]
        s_score = sem("s_score")
        s_ldif = sem("s_ldif")
        s_dense = sem("s_dense")
        s_scoreT_ps = sem("s_scoreT_ps")
        s_scoreT = sem("s_scoreT")
        s_db_ps = sem("s_db_ps")
        s_db = sem("s_db")
        s_part = sem("s_part")
        s_sum = sem("s_sum")
        s_out = sem("s_out")

        xT_ps = [bank[c] for c in range(HC)]
        cond_ps = [bank[2 + c] for c in range(HC)]
        lg_ps = bank[4][:, 0:GT * E].rearrange("p (t e) -> p t e", t=GT)
        rank_ps = bank[5][:, 0:GT * E].rearrange("p (t e) -> p t e", t=GT)
        yn_ps = [bank[6 + i][:, :].rearrange("p (t h) -> p t h", t=2) for i in range(2)]
        scoreT_ps = [bank[g][0:3 * E, :] for g in range(NG)]
        db_ps = [bank[n][:, :].rearrange("p (t h) -> p t h", t=2) for n in (6, 7, 0, 1, 2, 3, 6, 7)]
        ygT_ps = [bank[i][:, :].rearrange("p (j c s) -> p j c s", j=2, c=HC) for i in range(2)]
        gu_ps = [bank[2 + i][:, :].rearrange("p (j f) -> p j f", j=2) for i in range(2)]
        actT_ps = [bank[4 + i][:, 0:2 * P].rearrange("p (j s) -> p j s", j=2) for i in range(2)]
        dn_ps = [bank[6 + i][:, :].rearrange("p (j h) -> p j h", j=2) for i in range(2)]

        block = ctx.enter_context(nc.Block())

        def need(eng, semaphore, value):
            if not isinstance(value, int) or value > 0:
                eng.wait_ge(semaphore, value)

        def table_values(engine, row, start, n, top_value):
            return nc.values_load_multi_w_load_instructions(
                table[0:1, row, bass.ds(start, n)], engines=[engine], min_val=0, max_val=top_value,
                skip_runtime_bounds_check_because="the table's rows and experts come from counts that sum to "
                                                  "the number of pairs, whatever the inputs")[1]

        halves = [[range(t, t + GT // 2) for t in (g * GT, g * GT + GT // 2)] for g in range(NG)]

        def first_choices_placed(engine, g):
            for h in range(2):
                engine.wait_ge(s_first[g][h], 16 * GT // 2)

        def xT_copies(g, c):
            return g * HC + c + (1 if g == 0 and c == 0 else 0)

        def earlier(i, u, n):
            return (i, u - n) if u >= n else (i - 1, u - n + PAIRS_IN_BODY)

        @block.sync
        def _(sp):
            sp.dma_start(fs_nat[:, :, :, :], fside.rearrange("b a (c p) r -> p (b a) c r", p=P)).then_inc(s_side_in, 16)
            sp.dma_start(w_nat[:, :, :], cond_w.rearrange("(c p) i -> p c i", p=P)).then_inc(s_w_in, 16)

            def load_x(g):
                sp.dma_start(x_sb[:, g * GT:(g + 1) * GT, :], x_v[:, g * GT:(g + 1) * GT, :]).then_inc(s_x[g], 16)

            load_x(0)
            sp.dma_start(fcb[:, :], fc_bias.rearrange("(c p) -> p c", p=P),
                         allow_slow_non_contiguous=True).then_inc(s_bias_in, 16)
            for b in range(B):
                sp.dma_start(cnd[:, b, :], cond[b, :].rearrange("(c p) -> p c", p=P),
                             allow_slow_non_contiguous=True).then_inc(s_bias_in, 16)
            load_x(1)
            sp.dma_start(rw[:, :, :], router_w.rearrange("(c p) e -> p c e", p=P)).then_inc(s_router_in, 16)
            for g in range(2, NG):
                load_x(g)
            sp.dma_start(braw[:, 0, :], gate_up_bias).then_inc(s_eb, 16)
            sp.dma_start(braw[:, 1, :], down_bias).then_inc(s_eb, 16)

            def load_weights(e):
                gu, dn = slice(e * HC * F2, (e + WE) * HC * F2), slice(e * H, (e + WE) * H)
                sp.dma_start(wgu_raw[:, gu].rearrange("p (e c f) -> p (e c) f", c=HC, f=F2),
                             gate_up[e:e + WE, :, :].rearrange("e (c p) f -> p (e c) f", p=P)
                             ).then_inc(s_w[e // WE], 16)
                sp.dma_start(wd_raw[:, dn].rearrange("p (e h) -> p e h", h=H),
                             down[e:e + WE, :, :].rearrange("e p h -> p e h")).then_inc(s_w[e // WE], 16)

            def prefill(e, n):
                sp.dma_start(xs[e * REGION:(e + n) * REGION, :].rearrange("(e r) c -> r e c", r=REGION)[0:P, :, :],
                             pad[:, :].unsqueeze(1).broadcast_to([P, n, RW])).then_inc(s_prefill, 16)

            for e in range(0, 4 * WE, WE):
                load_weights(e)
            sp.wait_ge(s_pad, 2)
            prefill(0, E // 4)
            first_choices_placed(sp, 0)
            load_weights(4 * WE)
            prefill(E // 4, E // 4)
            sp.wait_ge(s_bsplit, 2)
            for n, part in enumerate(("hi", "lo", "hi")):
                sp.dma_start(db3[n * E:(n + 1) * E, :].bitcast(FP32),
                             bsplit[part][:, 1, :].bitcast(FP32)).then_inc(s_db3, 16)
            for n, part in enumerate(PARTS):
                sp.dma_start(gub2[n * E:(n + 1) * E, :].bitcast(FP32),
                             bsplit[part][:, 0, :].bitcast(FP32)).then_inc(s_gub2, 16)
            first_choices_placed(sp, 1)
            for e in range(5 * WE, 7 * WE, WE):
                load_weights(e)
            first_choices_placed(sp, 2)
            load_weights(7 * WE)
            prefill(E // 2, E // 4)
            first_choices_placed(sp, 3)
            prefill(3 * E // 4, E // 4)
            sp.dma_start(xs[E * REGION:XROWS, :], pad[:, :]).then_inc(s_prefill, 16)

            def load_blocks(i, rows=None):
                rows = rows or table_values(mybir.EngineType.SP, 0, i * RING, RING, XROWS - P)
                for r in range(RING):
                    if r % 2 == 0:
                        need(sp, s_idx, (i - 1) * PAIRS_IN_BODY + r // 2 + 1)
                    sp.dma_start(yg[:, r, :], xs[bass.ds(rows[r], P), :]).then_inc(s_yg[r // 2], 16)

            sp.wait_ge(s_table, 1)
            rows = table_values(mybir.EngineType.SP, 0, 0, RING, XROWS - P)
            sp.wait_ge(s_prefill, 16 * 5)
            sp.wait_ge(s_second, 16 * NT)
            load_blocks(0, rows)
            with sp.Fori(1, ITERS) as i:
                load_blocks(i)

            for u in range(PAIRS_IN_BODY):
                sp.wait_ge(s_stored[u], 32 * ITERS)
            for g in range(NG):
                ts = slice(g * GT, (g + 1) * GT)
                sp.dma_start(yrow[:, ts, 0:H], rs_v[:, 0, ts, :]).then_inc(s_back[0][g], 16)
                half, h0 = (yg[:, :, 0:H], g * GT) if g < NG // 2 else (res, g * GT - RING)
                sp.dma_start(half[:, h0:h0 + GT, :], rs_v[:, 1, ts, :]).then_inc(s_back[1][g], 16)

        @block.gpsimd
        def _(pool):
            nc.gpsimd.memset(ident[:, :], 0.0).then_inc(s_ident0, 1)
            pool.wait_ge(s_ident0, 1)
            nc.gpsimd.affine_select(out=ident[:, :], in_=ident[:, :], compare_op=ALU.not_equal, fill=1.0,
                                    base=0, pattern=[[-1, P]], channel_multiplier=1).then_inc(s_ident, 1)
            nc.gpsimd.memset(pad[:, 0:H], 0.0).then_inc(s_pad, 1)
            nc.gpsimd.iota(pad[:, H:RW].bitcast(I32), pattern=[[0, 1]], base=SKIP,
                           channel_multiplier=0).then_inc(s_pad, 1)
            nc.gpsimd.memset(tri[:, :], 1.0).then_inc(s_const, 1)
            nc.gpsimd.memset(trif[:, :], 1.0).then_inc(s_const, 1)
            nc.gpsimd.memset(ones_b[:, :], 1.0).then_inc(s_const, 1)
            nc.gpsimd.memset(ones_f[:, :], 1.0).then_inc(s_const, 1)
            nc.gpsimd.memset(ecol[:, :], 0.0).then_inc(s_const, 1)
            nc.gpsimd.iota(iota_e[:, :], pattern=[[1, E]], base=0, channel_multiplier=0,
                           allow_small_or_imprecise_dtypes=True).then_inc(s_const, 1)
            nc.gpsimd.iota(ebase[:, :], pattern=[[REGION, E]], base=P, channel_multiplier=0,
                           allow_small_or_imprecise_dtypes=True).then_inc(s_const, 1)
            nc.gpsimd.iota(iota_blk[:, :], pattern=[[1, NB]], base=0, channel_multiplier=0,
                           allow_small_or_imprecise_dtypes=True).then_inc(s_const, 1)
            nc.gpsimd.iota(iota_cnt[:, :], pattern=[[P, NT]], base=0, channel_multiplier=0,
                           allow_small_or_imprecise_dtypes=True).then_inc(s_const, 1)
            pool.wait_ge(s_const, 9)
            nc.gpsimd.affine_select(out=tri[:, :], in_=tri[:, :], compare_op=ALU.is_gt, fill=0.0,
                                    base=0, pattern=[[1, P]], channel_multiplier=-1).then_inc(s_const, 1)
            nc.gpsimd.affine_select(out=trif[:, :], in_=trif[:, :], compare_op=ALU.is_gt, fill=0.0,
                                    base=0, pattern=[[1, E1]], channel_multiplier=-1).then_inc(s_const, 1)
            nc.gpsimd.iota(ecol[:, 0:1], pattern=[[0, 1]], base=0, channel_multiplier=REGION,
                           allow_small_or_imprecise_dtypes=True).then_inc(s_const, 1)
            nc.gpsimd.affine_select(out=ecol[:, 1:2], in_=ecol[:, 1:2], compare_op=ALU.is_ge, fill=float(P),
                                    base=-E, pattern=[[0, 1]], channel_multiplier=1).then_inc(s_const, 1)
            nc.gpsimd.iota(ecol[:, 2:3], pattern=[[0, 1]], base=0, channel_multiplier=1,
                           allow_small_or_imprecise_dtypes=True).then_inc(s_const, 1)
            nc.gpsimd.affine_select(out=ecol[:, 3:4], in_=ecol[:, 3:4], compare_op=ALU.is_gt, fill=float(NB),
                                    base=E, pattern=[[0, 1]], channel_multiplier=-1).then_inc(s_const, 1)
            pool.wait_ge(s_const, 15)
            nc.gpsimd.affine_select(out=ecol[:, 2:3], in_=ecol[:, 2:3], compare_op=ALU.is_gt, fill=0.0,
                                    base=E, pattern=[[0, 1]], channel_multiplier=-1).then_inc(s_const, 1)
            nc.gpsimd.iota(yrow[:, :, H].bitcast(I32), pattern=[[P, NT]], base=0,
                           channel_multiplier=1).then_inc(s_dest, 1)

            def scatter(ts, k, done):
                for t in ts:
                    nc.gpsimd.indirect_dma_start(
                        out=xs, out_offset=bass.IndirectOffsetOnAxis(ap=slot[:, t, k:k + 1], axis=0),
                        in_=yrow[:, t, :], in_offset=None).then_inc(done, 16)

            pool.wait_ge(s_dest, 1)
            for g in range(NG):
                pool.wait_ge(s_slot, g + 1)
                for h in range(2):
                    pool.wait_ge(s_yn, 2 * g + h + 1)
                    scatter(halves[g][h], 0, s_first[g][h])
                for h in range(2):
                    pool.wait_ge(s_first[g][h], 16 * GT // 2)
                    dest = yrow[:, halves[g][h].start:halves[g][h].stop, H].bitcast(I32)
                    nc.gpsimd.tensor_scalar(dest, dest, float(T), None, ALU.add).then_inc(s_dest, 1)
                    pool.wait_ge(s_dest, 2 * g + h + 2)
                    scatter(halves[g][h], 1, s_second)

            last_row = pool.to_reg(SKIP - 1)
            pairs_wanted = pool.alloc_register("pairs_wanted")
            pool.reg_mov(pairs_wanted, 0)

            def store_blocks():
                for s in range(RING):
                    if s % 2 == 0:
                        pool.reg_add(pairs_wanted, pairs_wanted, 1)
                    pool.wait_ge(s_dest, 2 * NG + 1)
                    pool.wait_ge(s_res, pairs_wanted)
                    nc.gpsimd.indirect_dma_start(
                        out=rs, out_offset=bass.IndirectOffsetOnAxis(ap=idx[:, s:s + 1], axis=0),
                        in_=res[:, s, :], in_offset=None,
                        bounds_check=last_row, oob_is_err=False).then_inc(s_stored[s // 2], 16)

            with pool.Fori(0, ITERS):
                store_blocks()

        @block.scalar
        def _(act_e):
            act_e.preload_act_table(ACT.Gelu)

            act_e.wait_ge(s_fsT_ps, 1)
            nc.scalar.activation(fsT[:, :, :], bank[4][0:R, :].rearrange("r (b h) -> r b h", b=B),
                                 ACT.Copy).then_inc(s_fsT, 1)
            act_e.wait_ge(s_wT_ps, 1)
            nc.scalar.activation(wT[:, :, :], bank[5][:, :].rearrange("p (c h) -> p c h", c=HC),
                                 ACT.Copy).then_inc(s_wT, 1)

            act_e.wait_ge(s_xT_ps, HC)
            nc.scalar.activation(xT[:, 0, 1, :], xT_ps[1][:, :], ACT.Copy).then_inc(s_xT_act, 1)

            act_e.wait_ge(s_cbias, 1)
            for g in range(NG):
                for oc in range(HC):
                    act_e.wait_ge(s_cond, g * HC + oc + 1)
                    if g >= 2 and oc == 0:
                        act_e.wait_ge(s_yn_ps, 2 * (g - 1))
                    nc.scalar.activation(yT[:, g % 2, oc, :], cond_ps[oc][:, :], ACT.Gelu,
                                         bias=cbias[:, g // GPB, oc:oc + 1]).then_inc(s_yT, 1)
                for h in range(2):
                    act_e.wait_ge(s_yn_ps, 2 * g + h + 1)
                    t = g * GT + 2 * h
                    nc.scalar.activation(yrow[:, t:t + 2, 0:H], yn_ps[h], ACT.Copy).then_inc(s_yn, 1)
                if g == NG - 1:
                    act_e.wait_ge(s_ldif, 1)
                    nc.scalar.activation(score[:, 0, :], ldif[:, :], ACT.Sigmoid).then_inc(s_score, 1)
                    nc.scalar.activation(score[:, 1, :], ldif[:, :], ACT.Sigmoid, scale=-1.0).then_inc(s_score, 1)
                for e in SPLIT_AFTER[g]:
                    act_e.wait_ge(s_w[e // WE], 32)
                    gu, dn = slice(e * HC * F2, (e + WE) * HC * F2), slice(e * H, (e + WE) * H)
                    nc.scalar.activation(wgu["hi"][:, gu], wgu_raw[:, gu], ACT.Copy).then_inc(s_whi, 1)
                    nc.scalar.activation(wd["hi"][:, dn], wd_raw[:, dn], ACT.Copy).then_inc(s_whi, 1)
            act_e.preload_act_table(ACT.Gelu_apprx_sigmoid)
            for g in range(NG):
                act_e.wait_ge(s_scoreT_ps, g + 1)
                nc.scalar.activation(scoreT[g // 2][:, g % 2 * GT * P:(g % 2 + 1) * GT * P], scoreT_ps[g],
                                     ACT.Copy).then_inc(s_scoreT, 1)

            for n in range(E // 2):
                act_e.wait_ge(s_gu_bias_ps, n + 1)
                nc.scalar.activation(gu_bias[:, n * 2 * F2:(n + 1) * 2 * F2], bank[4 + n % 2][:, :],
                                     ACT.Copy).then_inc(s_gu_bias, 1)

            def y_hi(p, u):
                act_e.wait_ge(s_ygT_ps, p + 1)
                need(act_e, s_gu, p - 1)
                nc.scalar.activation(ygT["hi"][:, u % 2], ygT_ps[u % 2], ACT.Copy).then_inc(s_yhi, 1)

            def act_hi(p, u):
                act_e.wait_ge(s_actT_ps, p + 1)
                need(act_e, s_dn, p - 1)
                nc.scalar.activation(actT["hi"][:, u % 2], actT_ps[u % 2], ACT.Copy).then_inc(s_ahi, 1)

            def gelu_sigmoid(p, u):
                act_e.wait_ge(s_gub, p + 1)
                need(act_e, s_act, p - 1)
                nc.scalar.activation(glu[:, u % 2], gub[:, u % 2, :, 0:F2:2],
                                     ACT.Gelu_apprx_sigmoid).then_inc(s_glu, 1)

            def copy_res(i, u):
                act_e.wait_ge(s_dn, i * PAIRS_IN_BODY + u + 1)
                nc.scalar.activation(res[:, 2 * u:2 * u + 2, :], dn_ps[u % 2], ACT.Copy).then_inc(s_res, 1)

            def copy_index(i, u):
                need(act_e, s_stored[u], 32 * i)
                nc.scalar.copy(idx[:, 2 * u:2 * u + 2], yg[:, 2 * u:2 * u + 2, H].bitcast(U32)).then_inc(s_idx, 1)

            def experts(i, first=False, last=False):
                for u in range(PAIRS_IN_BODY):
                    p = i * PAIRS_IN_BODY + u
                    if not (last and u == PAIRS_IN_BODY - 1):
                        y_hi(p + 1, u + 1)
                    if not (first and u == 0):
                        copy_index(*earlier(i, u, 1))
                    if not (first and u <= 2):
                        copy_res(*earlier(i, u, 3))
                    if not (first and u == 0):
                        act_hi(p - 1, u - 1)
                    gelu_sigmoid(p, u)

            y_hi(0, 0)
            experts(0, first=True)
            with act_e.Fori(1, ITERS - 1) as i:
                experts(i)
            experts(ITERS - 1, last=True)
            copy_res(ITERS - 1, PAIRS_IN_BODY - 3)
            copy_index(ITERS - 1, PAIRS_IN_BODY - 1)
            act_hi(ITERS * PAIRS_IN_BODY - 1, PAIRS_IN_BODY - 1)
            copy_res(ITERS - 1, PAIRS_IN_BODY - 2)
            copy_res(ITERS - 1, PAIRS_IN_BODY - 1)

            for t in range(0, NT, 2):
                act_e.wait_ge(s_sum, t + 2)
                act_e.dma_start(out_v[:, t:t + 2, :], x_sb[:, t:t + 2, :]).then_inc(s_out, 16)
            act_e.wait_ge(s_out, 16 * NT // 2)

        @block.tensor
        def _(pe):
            def warm_up(n, spare):
                for _ in range(n):
                    nc.tensor.transpose(spare[:, 0:P], ident[:, :], ident[:, :])

            pe.wait_ge(s_ident, 1)
            warm_up(WARM_START, bank[3])
            pe.wait_ge(s_side_in, 16)
            for b in range(B):
                for c in range(HC):
                    last = nc.tensor.transpose(bank[4][0:R, (b * HC + c) * P:(b * HC + c + 1) * P],
                                               fs_nat[:, b, c, :], ident[:, :])
            last.then_inc(s_fsT_ps, 1)
            pe.wait_ge(s_w_in, 16)
            for ic in range(HC):
                for oc in range(HC):
                    last = nc.tensor.transpose(bank[5][:, ic * H + oc * P:ic * H + (oc + 1) * P],
                                               w_nat[:, oc, ic * P:(ic + 1) * P], ident[:, :])
            last.then_inc(s_wT_ps, 1)
            def side_product(b):
                pe.wait_ge(s_fsT, 2)
                for ic in range(HC):
                    last = nc.tensor.matmul(bank[6 + b][:, ic * H:(ic + 1) * H], fsTs[:, b, ic * P:(ic + 1) * P],
                                            fsT[:, b, :], start=True, stop=True)
                last.then_inc(s_side_ps, 1)

            def transpose_x(g):
                pe.wait_ge(s_x[g], 16)
                for c in range(HC):
                    if g == 1 and c == 1:
                        pe.wait_ge(s_xT_act, 1)
                    elif g >= 1:
                        pe.wait_ge(s_xT, xT_copies(g - 1, c))
                    for q in range(GT):
                        last = nc.tensor.transpose(xT_ps[c][:, q * P:(q + 1) * P],
                                                   x_sb[:, g * GT + q, c * P:(c + 1) * P], ident[:, :])
                    last.then_inc(s_xT_ps, 1)

            def cond_product(g):
                pe.wait_ge(s_xT, xT_copies(g, HC - 1))
                if g == 0:
                    pe.wait_ge(s_xT_act, 1)
                for oc in range(HC):
                    if g >= 1:
                        pe.wait_ge(s_yT, (g - 1) * HC + oc + 1)
                    for ic in range(HC):
                        last = nc.tensor.matmul(cond_ps[oc][:, :], weff[:, g // GPB, ic, oc * P:(oc + 1) * P],
                                                xT[:, g % 2, ic, :], start=(ic == 0), stop=(ic == HC - 1))
                    last.then_inc(s_cond, 1)

            def logits(g):
                pe.wait_ge(s_yT, (g + 1) * HC)
                if g >= 1:
                    pe.wait_ge(s_lg, g)
                for q in range(GT):
                    for c in range(HC):
                        last = nc.tensor.matmul(lg_ps[:, q, :], yT[:, g % 2, c, q * P:(q + 1) * P], rw[:, c, :],
                                                start=(c == 0), stop=(c == HC - 1))
                last.then_inc(s_lg_ps, 1)

            def y_by_token(g):
                for h in range(2):
                    if g >= 1:
                        pe.wait_ge(s_yn, 2 * (g - 1) + h + 1)
                    for j in range(2):
                        q = 2 * h + j
                        for c in range(HC):
                            last = nc.tensor.transpose(yn_ps[h][:, j, c * P:(c + 1) * P],
                                                       yT[:, g % 2, c, q * P:(q + 1) * P], ident[:, :])
                    last.then_inc(s_yn_ps, 1)

            def ranks(g):
                pe.wait_ge(s_gsum, g + 1)
                if g >= 1:
                    pe.wait_ge(s_slot, g)
                nc.tensor.matmul(rank_ps, tri[:, :], multi[:, :, 0:E], start=True, stop=False)
                for q in range(GT - 1):
                    n = GT - 1 - q
                    last = nc.tensor.matmul(rank_ps[:, q + 1:GT, :], ones_b[:, :],
                                            multi[:, q:q + 1, 0:E].broadcast_to([P, n, E]),
                                            start=False, stop=(g == 0 and q == GT - 2))
                for j in range(g):
                    last = nc.tensor.matmul(rank_ps, ones_b[:, :], gsum[:, j:j + 1, 0:E].broadcast_to([P, GT, E]),
                                            start=False, stop=(j == g - 1))
                last.then_inc(s_rank, 1)

            warm_up(WARM_W, bank[3])
            side_product(0)
            transpose_x(0)
            side_product(1)
            pe.wait_ge(s_weff, 1)
            cond_product(0)
            transpose_x(1)
            pe.wait_ge(s_router_in, 16)
            pe.wait_ge(s_weff, B)
            pe.wait_ge(s_const, 16)
            for g in range(NG):
                logits(g)
                y_by_token(g)
                if g < NG - 1:
                    warm_up(WARM_GAP, bank[3])
                ranks(g)
                if g + 1 < NG:
                    cond_product(g + 1)
                if g + 2 < NG:
                    transpose_x(g + 2)

            pe.wait_ge(s_slot, NG)
            for g in range(NG):
                last = nc.tensor.matmul(bank[5][0:E1, 128:129], gsum[:, g, :], ones_b[:, 0:1],
                                        start=(g == 0), stop=(g == NG - 1))
            last.then_inc(s_cnt, 1)
            pe.wait_ge(s_nblk, 1)
            nc.tensor.matmul(bank[5][0:E1, 136:137], trif[:, :], nblk[:, :], start=True, stop=True).then_inc(s_pre, 1)
            pe.wait_ge(s_dense, 1)
            for t in range(NT):
                last = nc.tensor.transpose(scoreT_ps[t // GT][:, (t % GT) * P:(t % GT + 1) * P], dense3[:, t, :, :],
                                           ident[:, :])
                if t % GT == GT - 1:
                    last.then_inc(s_scoreT_ps, 1)
            pe.wait_ge(s_own, 1)
            nc.tensor.matmul(bank[5][0:1, 144:144 + NB], ones_f[:, 0:1], rowown[:, :], start=True, stop=True)
            nc.tensor.matmul(bank[5][0:1, 208:208 + NB], ecol[:, 2:3], owner[:, :],
                             start=True, stop=True).then_inc(s_tab_ps, 1)

            warm_up(WARM_BIAS, bank[4])
            pe.wait_ge(s_db3, 48)
            pe.wait_ge(s_yn, 2 * NG)
            pe.wait_ge(s_scoreT, NG)

            def spread_biases(n):
                if n >= 2:
                    pe.wait_ge(s_gu_bias, n - 1)
                    warm_up(WARM_SPREAD, bank[4 + n % 2])
                for j in range(2):
                    e = 2 * n + j
                    last = nc.tensor.matmul(bank[4 + n % 2][:, j * F2:(j + 1) * F2],
                                            sel[:, e:e + 1].broadcast_to([2 * E, P]), gub2[:, :],
                                            start=True, stop=True)
                last.then_inc(s_gu_bias_ps, 1)

            pe.wait_ge(s_gub2, 32)
            pe.wait_ge(s_sel, 1)
            pe.wait_ge(s_table, 1)
            for k in range(NT // 2):
                for n in range(k * E // NT, (k + 1) * E // NT):
                    spread_biases(n)
                if k >= 6:
                    pe.wait_ge(s_db, k - 5)
                for t in range(2 * k, 2 * k + 2):
                    last = nc.tensor.matmul(db_ps[k][:, t % 2, :],
                                            scoreT[t // RING][:, t % RING * P:(t % RING + 1) * P], db3[:, :],
                                            start=True, stop=True)
                last.then_inc(s_db_ps, 1)

            owners = table_values(mybir.EngineType.PE, 1, 0, RING, E - 1)
            pe.wait_ge(s_wlo, E // WE)
            pe.wait_ge(s_db, NT // 2 - 2)
            TERMS = (("hi", "hi"), ("hi", "lo"), ("lo", "hi"))

            def transpose_y(i, u):
                pe.wait_ge(s_yg[u], 32 * i + 32)
                for j in range(2):
                    for c in range(HC):
                        last = nc.tensor.transpose(ygT_ps[u % 2][:, j, c, :], yg[:, 2 * u + j, c * P:(c + 1) * P],
                                                   ident[:, :])
                last.then_inc(s_ygT_ps, 1)

            def gate_up_product(i, u, owners):
                pe.wait_ge(s_ylo, i * PAIRS_IN_BODY + u + 1)
                for j in range(2):
                    e = owners[j]
                    o = gu_ps[u % 2][:, j, :]
                    for c in range(HC):
                        for n, (yp, wp) in enumerate(TERMS):
                            last = nc.tensor.matmul(o, ygT[yp][:, u % 2, j, c, :],
                                                    wgu[wp][:, bass.ds(e * (HC * F2) + c * F2, F2)],
                                                    start=(c == 0 and n == 0),
                                                    stop=(c == HC - 1 and n == len(TERMS) - 1))
                last.then_inc(s_gu, 1)

            def transpose_act(i, u):
                pe.wait_ge(s_act, i * PAIRS_IN_BODY + u + 1)
                for j in range(2):
                    last = nc.tensor.transpose(actT_ps[u % 2][:, j, :], act[:, u % 2, j, :], ident[:, :])
                last.then_inc(s_actT_ps, 1)

            def down_product(i, u, owners):
                p = i * PAIRS_IN_BODY + u
                pe.wait_ge(s_alo, p + 1)
                need(pe, s_res, p - 1)
                for j in range(2):
                    e = owners[j]
                    o = dn_ps[u % 2][:, j, :]
                    for n, (ap, wp) in enumerate(TERMS):
                        last = nc.tensor.matmul(o, actT[ap][:, u % 2, j, :], wd[wp][:, bass.ds(e * H, H)],
                                                start=(n == 0), stop=(n == len(TERMS) - 1))
                last.then_inc(s_dn, 1)

            def experts(i, owners=None, first=False, last=False):
                end = PAIRS_IN_BODY - 1
                back = 0 if first else 4
                owners = owners or table_values(mybir.EngineType.PE, 1, i * RING - back, RING + back, E - 1)
                for u in range(PAIRS_IN_BODY):
                    if u < end:
                        transpose_y(i, u + 1)
                    elif not last:
                        transpose_y(i + 1, 0)
                    at = back + 2 * u
                    gate_up_product(i, u, owners[at:at + 2])
                    if not (first and u == 0):
                        transpose_act(*earlier(i, u, 1))
                    if first and u == 2:
                        pe.wait_ge(s_db, NT // 2)
                    if not (first and u <= 1):
                        down_product(*earlier(i, u, 2), owners[at - 4:at - 2])

            transpose_y(0, 0)
            warm_up(WARM_EXPERTS, bank[3])
            experts(0, owners, first=True)
            with pe.Fori(1, ITERS - 1) as i:
                experts(i)
            experts(ITERS - 1, last=True)
            owners = table_values(mybir.EngineType.PE, 1, NB - 4, 4, E - 1)
            down_product(ITERS - 1, PAIRS_IN_BODY - 2, owners[0:2])
            transpose_act(ITERS - 1, PAIRS_IN_BODY - 1)
            down_product(ITERS - 1, PAIRS_IN_BODY - 1, owners[2:4])

        @block.vector
        def _(dve):
            own_steps = [0]

            def after(ins):
                own_steps[0] += 1
                ins.then_inc(s_v, 1)
                dve.wait_ge(s_v, own_steps[0])

            dve.wait_ge(s_fsT, 1)
            nc.vector.tensor_scalar(fsTs[:, :, :], fsT[:, :, :], 1.0 / (H * R), None, ALU.mult).then_inc(s_fsT, 1)

            def add_side(b):
                dve.wait_ge(s_side_ps, b + 1)
                dve.wait_ge(s_wT, 1)
                nc.vector.tensor_tensor(weff[:, b, :, :], bank[6 + b][:, :].rearrange("p (c h) -> p c h", c=HC),
                                        wT[:, :, :], ALU.add).then_inc(s_weff, 1)

            def split_biases():
                dve.wait_ge(s_eb, 32)
                ups = braw[:, 0, 1:F2:2]
                nc.vector.tensor_scalar(ups, ups, 1.0, None, ALU.add).then_inc(s_ups, 1)
                dve.wait_ge(s_ups, 1)
                nc.vector.tensor_copy(bsplit["hi"][:, :, :], braw[:, :, :]).then_inc(s_bsplit, 1)
                dve.wait_ge(s_bsplit, 1)
                nc.vector.tensor_tensor(bsplit["lo"][:, :, :], braw[:, :, :], bsplit["hi"][:, :, :].bitcast(FP32),
                                        ALU.subtract).then_inc(s_bsplit, 1)
                nc.vector.tensor_tensor(sel[:, :], ident[0:2 * E, 0:E], ident[0:2 * E, E:2 * E],
                                        ALU.add).then_inc(s_sel, 1)

            def split_weights(experts):
                for e in experts:
                    dve.wait_ge(s_whi, 2 * (e // WE + 1))
                    gu, dn = slice(e * HC * F2, (e + WE) * HC * F2), slice(e * H, (e + WE) * H)
                    nc.vector.tensor_tensor(wgu["lo"][:, gu], wgu_raw[:, gu], wgu["hi"][:, gu].bitcast(FP32),
                                            ALU.subtract)
                    nc.vector.tensor_tensor(wd["lo"][:, dn], wd_raw[:, dn], wd["hi"][:, dn].bitcast(FP32),
                                            ALU.subtract).then_inc(s_wlo, 1)

            def copy_xT(g):
                for c in range(HC if g else 1):
                    dve.wait_ge(s_xT_ps, g * HC + c + 1)
                    if g >= 2:
                        dve.wait_ge(s_cond, (g - 1) * HC)
                    nc.vector.tensor_copy(xT[:, g % 2, c, :], xT_ps[c][:, :]).then_inc(s_xT, 1)

            def choose(g):
                ts = slice(g * GT, (g + 1) * GT)
                dve.wait_ge(s_lg_ps, g + 1)
                nc.vector.tensor_copy(lg[:, ts, :], lg_ps).then_inc(s_lg, 1)
                dve.wait_ge(s_lg, g + 1)
                for t in range(g * GT, (g + 1) * GT):
                    last = nc.vector.max(top[:, t, :], lg[:, t, :])
                after(last)
                for t in range(g * GT, (g + 1) * GT):
                    last = nc.vector.max_index(topi[:, t, :], top[:, t, :], lg[:, t, :])
                after(last)
                if g >= 1:
                    dve.wait_ge(s_rank, g)
                after(nc.vector.tensor_tensor(
                    mask[:, :, :, :], topi[:, ts, 0:TOPK].unsqueeze(3).broadcast_to([P, GT, TOPK, E]),
                    iota_e[:, :].unsqueeze(1).unsqueeze(1).broadcast_to([P, GT, TOPK, E]), ALU.is_equal))
                after(nc.vector.tensor_tensor(multi[:, :, 0:E], mask[:, :, 0, :], mask[:, :, 1, :], ALU.add))
                with nc.allow_low_precision("counts up to 8 are exact"):
                    nc.vector.tensor_reduce(gsum[:, g, :], multi[:, :, :].rearrange("p t e -> p e t"),
                                            axis=AX.X, op=ALU.add).then_inc(s_gsum, 1)

            def place(g):
                ts = slice(g * GT, (g + 1) * GT)
                dve.wait_ge(s_rank, g + 1)
                after(nc.vector.tensor_tensor(rbase[:, :, :], rank_ps,
                                              ebase[:, :].unsqueeze(1).broadcast_to([P, GT, E]), ALU.add))
                after(nc.vector.tensor_tensor(prod[:, :, :, :], mask[:, :, :, :],
                                              rbase[:, :, :].unsqueeze(2).broadcast_to([P, GT, TOPK, E]), ALU.mult))
                with nc.allow_low_precision("row numbers are integers below 2^24"):
                    nc.vector.tensor_reduce(slot[:, ts, :], prod[:, :, :, :], axis=AX.X, op=ALU.add).then_inc(s_slot, 1)

            add_side(0)
            copy_xT(0)
            dve.wait_ge(s_bias_in, 16 * (1 + B))
            for b in range(B):
                last = nc.vector.tensor_tensor(cbias[:, b, :], cnd[:, b, :], fcb[:, :], ALU.add)
            last.then_inc(s_cbias, 1)
            add_side(1)
            dve.wait_ge(s_const, 16)
            nc.vector.memset(multi[:, :, :], 0.0).then_inc(s_multi, 1)
            dve.wait_ge(s_multi, 1)
            copy_xT(1)
            for g in range(NG):
                choose(g)
                place(g)
                if g == 0:
                    split_biases()
                if g < NG - 1:
                    split_weights(SPLIT_AFTER[g])
                if g + 2 < NG:
                    copy_xT(g + 2)
            nc.vector.tensor_tensor(ldif[:, :], top[:, :, 0], top[:, :, 1], ALU.subtract).then_inc(s_ldif, 1)

            dve.wait_ge(s_cnt, 1)
            after(nc.vector.tensor_copy(cnt[:, :], bank[5][0:E1, 128:129]))
            after(nc.vector.tensor_scalar(over[:, :], iota_cnt[:, :], cnt[:, 0:1], None, ALU.is_lt))
            after(nc.vector.tensor_reduce(nblk[:, :], over[:, :], axis=AX.X, op=ALU.add))
            nc.vector.tensor_tensor(nblk[:, :], nblk[:, :], ecol[:, 3:4], ALU.add).then_inc(s_nblk, 1)
            every = [P, NT, TOPK, E]
            after(nc.vector.tensor_tensor(chosen[:, :, :, :], topi[:, :, 0:TOPK].unsqueeze(3).broadcast_to(every),
                                          iota_e[:, :].unsqueeze(1).unsqueeze(1).broadcast_to(every), ALU.is_equal))
            dve.wait_ge(s_score, 2)
            after(nc.vector.tensor_tensor(chosen[:, :, :, :], chosen[:, :, :, :],
                                          score[:, :, :].rearrange("p k t -> p t k").unsqueeze(3).broadcast_to(every),
                                          ALU.mult))
            after(nc.vector.tensor_tensor(dense[:, :, :], chosen[:, :, 0, :], chosen[:, :, 1, :], ALU.add))
            nc.vector.tensor_copy(dense3[:, :, 0, :].bitcast(FP32R), dense[:, :, :])
            after(nc.vector.tensor_copy(dense3[:, :, 1, :].bitcast(FP32R), dense[:, :, :]))
            nc.vector.tensor_tensor(dense3[:, :, 2, :], dense[:, :, :], dense3[:, :, 0, :],
                                    ALU.subtract).then_inc(s_dense, 1)
            late = SPLIT_AFTER[NG - 1]
            split_weights(late[0:1])
            dve.wait_ge(s_pre, 1)
            after(nc.vector.tensor_copy(cexc[:, :], bank[5][0:E1, 136:137]))
            after(nc.vector.tensor_tensor(cinc[:, :], cexc[:, :], nblk[:, :], ALU.add))
            after(nc.vector.tensor_tensor(base[:, :], cexc[:, :], ecol[:, 1:2], ALU.mult))
            after(nc.vector.tensor_tensor(base[:, :], base[:, :], cnt[:, :], ALU.add))
            after(nc.vector.tensor_tensor(base[:, :], base[:, :], ecol[:, 0:1], ALU.add))
            after(nc.vector.tensor_scalar(started[:, :], iota_blk[:, :], cexc[:, 0:1], None, ALU.is_ge))
            after(nc.vector.scalar_tensor_tensor(owner[:, :], iota_blk[:, :], cinc[:, 0:1], started[:, :],
                                                 ALU.is_lt, ALU.mult))
            after(nc.vector.tensor_scalar(rowat[:, :], iota_blk[:, :], ecol[:, 1:2], base[:, 0:1],
                                          ALU.mult, ALU.subtract))
            nc.vector.scalar_tensor_tensor(rowown[:, :], rowat[:, :], -1.0, owner[:, :],
                                           ALU.mult, ALU.mult).then_inc(s_own, 1)
            split_weights(late[1:2])
            dve.wait_ge(s_tab_ps, 1)
            after(nc.vector.tensor_copy(table[0:1, 0, :], bank[5][0:1, 144:144 + NB]))
            nc.vector.tensor_copy(table[0:1, 1, :], bank[5][0:1, 208:208 + NB]).then_inc(s_table, 1)

            split_weights(late[2:])
            for k in range(NT // 2):
                dve.wait_ge(s_db_ps, k + 1)
                xk = x_sb[:, 2 * k:2 * k + 2, :]
                nc.vector.tensor_tensor(xk, xk, db_ps[k], ALU.add).then_inc(s_db, 1)

            def y_lo(p, u):
                dve.wait_ge(s_yhi, p + 1)
                nc.vector.tensor_tensor(ygT["lo"][:, u % 2], ygT_ps[u % 2], ygT["hi"][:, u % 2].bitcast(FP32),
                                        ALU.subtract).then_inc(s_ylo, 1)

            def act_lo(p, u):
                dve.wait_ge(s_ahi, p + 1)
                nc.vector.tensor_tensor(actT["lo"][:, u % 2], actT_ps[u % 2], actT["hi"][:, u % 2].bitcast(FP32),
                                        ALU.subtract).then_inc(s_alo, 1)

            def add_bias(p, u, owners):
                dve.wait_ge(s_gu, p + 1)
                for j in range(2):
                    last = nc.vector.tensor_tensor(gub[:, u % 2, j, :], gu_ps[u % 2][:, j, :],
                                                   gu_bias[:, bass.ds(owners[j] * F2, F2)], ALU.add)
                last.then_inc(s_gub, 1)

            def activate(p, u):
                b = u % 2
                dve.wait_ge(s_gub, p + 1)
                nc.vector.tensor_scalar(up1[:, b], gub[:, b, :, 1:F2:2], 1.0 - LIMIT, 1.0 + LIMIT,
                                        ALU.max, ALU.min).then_inc(s_up1, 1)
                dve.wait_ge(s_up1, p + 1)
                dve.wait_ge(s_glu, p + 1)
                need(dve, s_actT_ps, p - 1)
                nc.vector.scalar_tensor_tensor(act[:, b], glu[:, b], GLU_MAX, up1[:, b],
                                               ALU.min, ALU.mult).then_inc(s_act, 1)

            def experts(i, first=False, last=False):
                owners = table_values(mybir.EngineType.DVE, 1, i * RING, RING, E - 1)
                for u in range(PAIRS_IN_BODY):
                    p = i * PAIRS_IN_BODY + u
                    if not (last and u == PAIRS_IN_BODY - 1):
                        y_lo(p + 1, u + 1)
                    add_bias(p, u, owners[2 * u:2 * u + 2])
                    if not (first and u == 0):
                        act_lo(p - 1, u - 1)
                    activate(p, u)

            y_lo(0, 0)
            dve.wait_ge(s_gu_bias, E // 2)
            experts(0, first=True)
            with dve.Fori(1, ITERS - 1) as i:
                experts(i)
            experts(ITERS - 1, last=True)
            act_lo(ITERS * PAIRS_IN_BODY - 1, PAIRS_IN_BODY - 1)

            for g in range(NG):
                for k in range(TOPK):
                    dve.wait_ge(s_back[k][g], 16)
                    for t in range(g * GT, (g + 1) * GT):
                        r = second(t) if k else yrow[:, t, 0:H]
                        last = nc.vector.scalar_tensor_tensor(x_sb[:, t, :], r, score[:, k, t:t + 1],
                                                              x_sb[:, t, :], ALU.mult, ALU.add)
                        if k == TOPK - 1:
                            last.then_inc(s_sum, 1)
                    if k == 0:
                        last.then_inc(s_part, 1)
                        dve.wait_ge(s_part, g + 1)


_INS = ["x", "fside_Bx1x1024x16_0", "cond_1024", "L0_cond_W", "L0_cond_fc_bias", "L0_ffn_router_weight",
        "L0_ffn_gate_up_proj", "L0_ffn_gate_up_proj_bias", "L0_ffn_down_proj", "L0_ffn_down_proj_bias"]


def kernel(**inputs):
    import numpy as np
    import concourse.bacc as bacc
    from concourse.bass_utils import run_bass_kernel_spmd

    nc = bacc.Bacc("TRN2", target_bir_lowering=False, num_devices=1)
    arrays, args = {}, []
    for name in _INS:
        a = np.ascontiguousarray(inputs[name])
        arrays[f"in_{name}"] = a
        args.append(nc.dram_tensor(f"in_{name}", a.shape, mybir.dt.from_np(a.dtype), kind="ExternalInput").ap())
    shape = inputs["x"].shape
    out = nc.dram_tensor("out", shape, FP32, kind="ExternalOutput").ap()
    adaln_moe_ffn(nc, *args, out)
    r = run_bass_kernel_spmd(nc, [arrays], core_ids=[0])
    return r.results[0]["out"]
```
